# Optimizing a Trainium2 kernel written in Bass

```python
import numpy as np
import jax
import jax.numpy as jnp

def _softmax(x, axis=-1):
    return jax.nn.softmax(x, axis=axis)

def _gelu(x):
    return jax.nn.gelu(x, approximate=True)

def _silu(x):
    return jax.nn.silu(x)

def _sigmoid(x):
    return jax.nn.sigmoid(x)

def _layernorm(x, axis=-1, eps=1e-05):
    m = jnp.mean(x, axis=axis, keepdims=True)
    v = jnp.var(x, axis=axis, keepdims=True)
    return (x - m) / jnp.sqrt(v + eps)

def _scatter_add(tgt, idx, src, axis=0):
    return tgt.at[idx].add(src)

def _segment_sum(src, seg, n):
    return jax.ops.segment_sum(src, seg, n)
kernel_name = 'mk_prb_d1_jaxref_r4_6e888b'

def setup_inputs(seed: int=0):
    np.random.seed(seed)
    _w = jnp.asarray

    def _L0_attn_setup():
        import jax, jax.numpy as jnp
        import numpy as np
        D_MODEL = 256
        N_HEADS = 16
        HEAD_DIM = D_MODEL // N_HEADS
        BATCH = 2
        SEQ = 512

        def _alibi_bias(seq_len, n_heads, dtype):
            slopes = 1.0 / 2.0 ** (jnp.arange(n_heads, dtype=dtype) / n_heads)
            rel = jnp.arange(seq_len, dtype=dtype)[None, :] - jnp.arange(seq_len, dtype=dtype)[:, None]
            return slopes[:, None, None] * rel[None, :, :]
        key = jax.random.key(seed)
        ks = jax.random.split(key, 9)
        s = 0.02
        return {'x': jax.random.normal(ks[0], (BATCH, SEQ, D_MODEL), dtype=jnp.float32), 'Wq': jax.random.normal(ks[1], (D_MODEL, D_MODEL), dtype=jnp.float32) * s, 'bq': jnp.zeros((D_MODEL,), dtype=jnp.float32), 'Wk': jax.random.normal(ks[2], (D_MODEL, D_MODEL), dtype=jnp.float32) * s, 'bk': jnp.zeros((D_MODEL,), dtype=jnp.float32), 'Wv': jax.random.normal(ks[3], (D_MODEL, D_MODEL), dtype=jnp.float32) * s, 'bv': jnp.zeros((D_MODEL,), dtype=jnp.float32), 'Wo': jax.random.normal(ks[4], (D_MODEL, D_MODEL), dtype=jnp.float32) * s, 'bo': jnpp_zeros() if False else jnp.zeros((D_MODEL,), dtype=jnp.float32)}
    _L0_attn_in = _L0_attn_setup()

    def _L0_ffn_setup():
        import jax, jax.numpy as jnp
        import numpy as np
        B, T, C = (4, 512, 256)
        E = 8
        K = 2
        H = 352
        HS = 352 * 2
        key = jax.random.key(seed)
        k = jax.random.split(key, 8)
        s = 0.02
        return {'x': jax.random.normal(k[0], (B, T, C), jnp.float32), 'Wg': jax.random.normal(k[1], (C, E), jnp.float32) * s, 'W1': jax.random.normal(k[2], (E, C, H), jnp.float32) * s, 'W2': jax.random.normal(k[3], (E, C, H), jnp.float32) * s, 'W3': jax.random.normal(k[4], (E, H, C), jnp.float32) * s, 'Ws1': jax.random.normal(k[5], (C, HS), jnp.float32) * s, 'Ws2': jax.random.normal(k[6], (C, HS), jnp.float32) * s, 'Ws3': jax.random.normal(k[7], (HS, C), jnp.float32) * s}
    _L0_ffn_in = _L0_ffn_setup()
    _d = {'L0_attn_x': _L0_attn_in['x'], 'L0_attn_Wq': _L0_attn_in['Wq'], 'L0_attn_bq': _L0_attn_in['bq'], 'L0_attn_Wk': _L0_attn_in['Wk'], 'L0_attn_bk': _L0_attn_in['bk'], 'L0_attn_Wv': _L0_attn_in['Wv'], 'L0_attn_bv': _L0_attn_in['bv'], 'L0_attn_Wo': _L0_attn_in['Wo'], 'L0_attn_bo': _L0_attn_in['bo'], 'L0_ffn_Wg': _L0_ffn_in['Wg'], 'L0_ffn_W1': _L0_ffn_in['W1'], 'L0_ffn_W2': _L0_ffn_in['W2'], 'L0_ffn_W3': _L0_ffn_in['W3'], 'L0_ffn_Ws1': _L0_ffn_in['Ws1'], 'L0_ffn_Ws2': _L0_ffn_in['Ws2'], 'L0_ffn_Ws3': _L0_ffn_in['Ws3']}
    _x0 = _d['L0_attn_x']
    _d['L0_attn_x'] = jax.random.normal(jax.random.fold_in(jax.random.key(seed), 1), (8, 1024, 256), dtype=_x0.dtype)
    del _x0
    return _d

def reference(L0_attn_x, L0_attn_Wq, L0_attn_bq, L0_attn_Wk, L0_attn_bk, L0_attn_Wv, L0_attn_bv, L0_attn_Wo, L0_attn_bo, L0_ffn_Wg, L0_ffn_W1, L0_ffn_W2, L0_ffn_W3, L0_ffn_Ws1, L0_ffn_Ws2, L0_ffn_Ws3):

    def _L0_attn_ref(x, Wq, bq, Wk, bk, Wv, bv, Wo, bo):
        import jax, jax.numpy as jnp
        import numpy as np
        D_MODEL = 256
        N_HEADS = 16
        HEAD_DIM = D_MODEL // N_HEADS
        BATCH = 2
        SEQ = 512

        def _alibi_bias(seq_len, n_heads, dtype):
            slopes = 1.0 / 2.0 ** (jnp.arange(n_heads, dtype=dtype) / n_heads)
            rel = jnp.arange(seq_len, dtype=dtype)[None, :] - jnp.arange(seq_len, dtype=dtype)[:, None]
            return slopes[:, None, None] * rel[None, :, :]
        B, S, D = x.shape
        H, Hd = (N_HEADS, HEAD_DIM)
        scale = Hd ** (-0.5)
        Q = (x @ Wq + bq).reshape(B, S, H, Hd)
        K = (x @ Wk + bk).reshape(B, S, H, Hd)
        V = (x @ Wv + bv).reshape(B, S, H, Hd)
        scores = jnp.einsum('bqhd,bkhd->bhqk', Q, K) * scale
        scores = scores + _alibi_bias(S, H, x.dtype)[None]
        attn = jax.nn.softmax(scores, axis=-1)
        out = jnp.einsum('bhqk,bkhd->bqhd', attn, V).reshape(B, S, D)
        return out @ Wo + bo

    def _L0_ffn_ref(x, Wg, W1, W2, W3, Ws1, Ws2, Ws3):
        import jax, jax.numpy as jnp
        import numpy as np
        B, T, C = (4, 512, 256)
        E = 8
        K = 2
        H = 352
        HS = 352 * 2
        b, t, c = x.shape
        xf = x.reshape(-1, c)
        n = xf.shape[0]
        router = xf @ Wg
        top_logits, idx = jax.lax.top_k(router, K)
        probs = jax.nn.softmax(top_logits.astype(jnp.float32), axis=-1).astype(x.dtype)
        w = jnp.zeros((n, E), x.dtype).at[jnp.arange(n)[:, None], idx].add(probs)
        h = jax.nn.silu(jnp.einsum('tc,ech->eth', xf, W1)) * jnp.einsum('tc,ech->eth', xf, W2)
        y = jnp.einsum('eth,ehc,te->tc', h, W3, w)
        y = y.reshape(b, t, c)
        hs = jax.nn.silu(xf @ Ws1) * (xf @ Ws2)
        y = y + (hs @ Ws3).reshape(b, t, c)
        return y
    x = L0_attn_x
    xn = _layernorm(x, axis=-1)
    x = x + _L0_attn_ref(xn, L0_attn_Wq, L0_attn_bq, L0_attn_Wk, L0_attn_bk, L0_attn_Wv, L0_attn_bv, L0_attn_Wo, L0_attn_bo) + _L0_ffn_ref(xn, L0_ffn_Wg, L0_ffn_W1, L0_ffn_W2, L0_ffn_W3, L0_ffn_Ws1, L0_ffn_Ws2, L0_ffn_Ws3)
    return x

_drawn_inputs = setup_inputs


def setup_inputs(seed=0):
    import zlib

    import numpy as np

    out = dict(_drawn_inputs(seed))
    spreads = {'L0_attn_bq': (0.0, 2.0),
     'L0_attn_bk': (0.0, 2.0),
     'L0_attn_bv': (0.0, 0.392),
     'L0_attn_bo': (0.0, 0.1)}
    factors = {'L0_attn_Wq': 8.0,
     'L0_attn_Wk': 8.0,
     'L0_ffn_Wg': 4.662,
     'L0_ffn_W1': 4.072,
     'L0_ffn_W2': 4.033,
     'L0_ffn_W3': 4.029,
     'L0_ffn_Ws1': 3.24,
     'L0_ffn_Ws2': 3.211,
     'L0_ffn_Ws3': 3.213}
    for name, (base, spread) in spreads.items():
        noise = np.random.default_rng([zlib.crc32(name.encode()), seed]).standard_normal(out[name].shape)
        drawn = base * np.exp(spread * noise) if base else spread * noise
        out[name] = jnp.asarray(drawn.astype(out[name].dtype))
    for name, factor in factors.items():
        out[name] = (out[name] * factor).astype(out[name].dtype)
    return out
```

```python
from contextlib import ExitStack

import numpy as np

import concourse.bass as bass
from concourse import mybir

F32 = mybir.dt.float32
F32R = mybir.dt.float32r
I32 = mybir.dt.int32
U32 = mybir.dt.uint32
ALU = mybir.AluOpType
ACT = mybir.ActivationFunctionType
AX = mybir.AxisListType

P = 128
NB, S, D = 8, 1024, 256
N = NB * S
NH, HD = 16, 16
NE, HE = 8, 352
HC = ((0, 128), (128, 128), (256, 96))
GT = 512
NG = N // GT
NT = N // P
NBLK = (2 * N - NE) // GT + NE
NSLOT = NBLK * GT
RAW = 4 * HE + 3 * D
W2_AT, W3_AT = 2 * HE, 4 * HE
SCALE = float(HD) ** -0.5
EPS = 1e-5


class Program:

    def __init__(self, nc, ctx):
        self.nc, self.ctx = nc, ctx
        self.queues = {e: [] for e in ("tensor", "vector", "scalar", "gpsimd", "sync")}
        self.sems, self.at, self.waited = {}, {}, {}

    def sem(self, name):
        if name not in self.sems:
            self.sems[name] = self.ctx.enter_context(self.nc.semaphore("s_" + name))
            self.at[name] = 0
        return self.sems[name]

    def wait(self, eng, *marks):
        for m in marks:
            if m is None:
                continue
            name, value = m
            if self.waited.get((eng, name), 0) < value:
                self.waited[eng, name] = value
                self.queues[eng].append(lambda e, s=self.sems[name], v=value: e.wait_ge(s, v))

    def put(self, eng, fn, *marks, sig=True):
        self.wait(eng, *marks)
        if not sig:
            self.queues[eng].append(fn)
            return None
        s = self.sem(eng)
        self.at[eng] += 1
        self.queues[eng].append(lambda e: fn(e).then_inc(s, 1))
        return eng, self.at[eng]

    def dma(self, eng, slot, out, in_, *marks, slow=False):
        self.wait(eng, *marks)
        s = self.sem(slot)
        self.at[slot] += 16
        self.queues[eng].append(
            lambda e: e.dma_start(out, in_, allow_slow_non_contiguous=slow).then_inc(s, 16))
        return slot, self.at[slot]

    def emit(self, block):
        for name, queue in self.queues.items():
            def run(e, queue=queue):
                for fn in queue:
                    fn(e)
            blocks = {"tensor": block.tensor, "vector": block.vector, "scalar": block.scalar,
                            "gpsimd": block.gpsimd, "sync": block.sync}
            blocks[name](run)


def build(nc, t, out):
    ctx = ExitStack()
    with ctx:
        pr = Program(nc, ctx)
        put, dma, wait = pr.put, pr.dma, pr.wait
        pe = lambda fn, *m, sig=False: put("tensor", fn, *m, sig=sig)
        dve = lambda fn, *m: put("vector", fn, *m)
        act = lambda fn, *m: put("scalar", fn, *m)
        pool = lambda fn, *m: put("gpsimd", fn, *m)

        def sbuf(stack, name, shape, dt=F32):
            return stack.enter_context(nc.sbuf_tensor(name, shape, dt))

        def dram(name, shape):
            return nc.dram_tensor(name, shape, F32).ap()

        ps = ctx.enter_context(nc.psum_tensor("ps", [P, 8, 512], F32))

        Xn = dram("Xn", [N, D])
        QKh = dram("QKh", [2 * D, N])
        QKl = dram("QKl", [2 * D, N])
        Vd = dram("Vd", [N, NH * 32])
        Akd = dram("Akd", [NH, 4, S])
        Aqd = dram("Aqd", [NH, 4, S])
        Wd = dram("Wd", [(NE + 2) * P, 2 * RAW])
        Xs = dram("Xs", [NSLOT, D])
        Ys = dram("Ys", [NSLOT, D])
        Od = dram("Od", [N, D])

        def mm(o, l, r, start, stop, *m, sig=False):
            return pe(lambda e: e.matmul(o, l, r, start=start, stop=stop), *m, sig=sig)

        def mm3(o, ks, *m, sig=False, first=True, last=True):
            wait("tensor", *m)
            n = 3 * len(ks)
            i = 0
            for lh, ll, rh, rl in ks:
                for l, r in ((ll, rh), (lh, rl), (lh, rh)):
                    end = i == n - 1
                    mark = mm(o, l, r, first and i == 0, last and end, sig=sig and end)
                    i += 1
            return mark

        def transpose(o, in_, *m, sig=False):
            return pe(lambda e: e.transpose(o, in_, ident[:, :]), *m, sig=sig)

        ident = sbuf(ctx, "ident", [P, P])
        WoH, WoL = (sbuf(ctx, n, [P, 2, D], F32R) for n in ("WoH", "WoL"))
        boc = sbuf(ctx, "boc", [P, 2])
        Lg = sbuf(ctx, "Lg", [P, NT, NE])
        prob = sbuf(ctx, "prob", [P, 2, NT])
        slot = sbuf(ctx, "slot", [P, 2, NT], I32)
        widx = sbuf(ctx, "widx", [P, NBLK], I32)
        xg = sbuf(ctx, "xg", [P, 2, 4, D])

        m_ident = dma("sync", "c_ident", ident[:, :], t["c_ident"])
        m_boc = dma("sync", "c_boc", boc[:, :], t["bo"].rearrange("(m p) -> p m", p=P), slow=True)

        A = ExitStack()
        Wst = sbuf(A, "Wst", [P, 2, 2, D])
        Wqk = {k: sbuf(A, "W" + k, [P, 2, 2, D], F32R) for k in ("h", "l")}
        Wvst = sbuf(A, "Wvst", [P, 2, D + NE])
        Wv = {k: sbuf(A, "Wv" + k, [P, 2, D + NE], F32R) for k in ("h", "l")}
        Wost = sbuf(A, "Wost", [P, 2, D])
        bqk = sbuf(A, "bqk", [P, 4])
        bvr = sbuf(A, "bvr", [P, D])
        ab = sbuf(A, "ab", [2 * NH, S])
        abh, abl = (sbuf(A, n, [2 * NH, S], F32R) for n in ("abh", "abl"))
        one = sbuf(A, "one", [2 * NH, S])
        zero = sbuf(A, "zero", [P, 8 * D])
        nhalf = sbuf(A, "nhalf", [P, 4])
        xt = sbuf(A, "xt", [P, 3, 4, D])
        stats = sbuf(A, "stats", [P, 2, 4, 6])
        mv = sbuf(A, "mv", [P, 2, 4, 2])
        veps = sbuf(A, "veps", [P, 2, 4])
        rstd = sbuf(A, "rstd", [P, 2, 4])
        xn = sbuf(A, "xn", [P, 2, 4, D])
        XH, XL = (sbuf(A, n, [P, 2, 2, GT], F32R) for n in ("XH", "XL"))
        qkH, qkL = (sbuf(A, n, [P, 2, 4, GT], F32R) for n in ("qkH", "qkL"))
        vs = sbuf(A, "vs", [P, 2, 4, NH, 32])
        wraw = sbuf(A, "wraw", [P, 2, RAW])
        wsp = sbuf(A, "wsp", [P, 2, 2 * RAW], F32R)

        def rows(w):
            return w.rearrange("(c p) n -> p c n", p=P)

        dma("sync", "c_w", Wst[:, 0, :, :], rows(t["Wq"]))
        dma("sync", "c_w", Wst[:, 1, :, :], rows(t["Wk"]))
        dma("sync", "c_w", Wvst[:, :, 0:D], rows(t["Wv"]))
        dma("sync", "c_w", Wvst[:, :, D:D + NE], rows(t["Wg"]))
        dma("sync", "c_w", Wost[:, :, :], rows(t["Wo"]))
        dma("sync", "c_w", bqk[:, 0:2], t["bq"].rearrange("(m p) -> p m", p=P), slow=True)
        dma("sync", "c_w", bqk[:, 2:4], t["bk"].rearrange("(m p) -> p m", p=P), slow=True)
        m_w = dma("sync", "c_w", bvr[:, :], t["bv"].rearrange("(a n) -> a n", a=1).broadcast_to([P, D]))

        m_nhalf = pool(lambda e: e.memset(nhalf[:, :], -0.5))
        m_bq = dve(lambda e: e.tensor_scalar(bqk[:, 0:2], bqk[:, 0:2], SCALE, None, ALU.mult), m_w)
        a1 = act(lambda e: e.activation(Wqk["h"][:, 0, :, :], Wst[:, 0, :, :], ACT.Copy, scale=SCALE), m_w)
        a2 = act(lambda e: e.copy(Wqk["h"][:, 1, :, :], Wst[:, 1, :, :]))
        a3 = act(lambda e: e.copy(Wv["h"][:, :, :], Wvst[:, :, :]))
        a4 = act(lambda e: e.copy(WoH[:, :, :], Wost[:, :, :]))
        m_wq = dve(lambda e: e.scalar_tensor_tensor(Wqk["l"][:, 0, :, :], Wst[:, 0, :, :], SCALE,
                                                    Wqk["h"][:, 0, :, :].bitcast(F32), ALU.mult, ALU.subtract), a1)
        m_wk = dve(lambda e: e.tensor_tensor(Wqk["l"][:, 1, :, :], Wst[:, 1, :, :],
                                             Wqk["h"][:, 1, :, :].bitcast(F32), ALU.subtract), a2)
        m_wv = dve(lambda e: e.tensor_tensor(Wv["l"][:, :, :], Wvst[:, :, :], Wv["h"][:, :, :].bitcast(F32),
                                             ALU.subtract), a3)
        m_wo = dve(lambda e: e.tensor_tensor(WoL[:, :, :], Wost[:, :, :], WoH[:, :, :].bitcast(F32),
                                             ALU.subtract), a4)

        v0 = pool(lambda e: e.memset(vs[:, :, :, :, :], 0.0))
        m_vs = pool(lambda e: e.memset(vs[:, :, :, :, HD:HD + 1], 1.0), v0)
        m_zero = pool(lambda e: e.memset(zero[:, :], 0.0))
        m_one = pool(lambda e: e.memset(one[:, :], 1.0))
        m_wz = pool(lambda e: e.memset(wraw[:, :, W3_AT + 2 * D:RAW], 0.0))

        m_ab = dma("sync", "c_ab", ab[:, :], t["c_alibi"])
        a5 = act(lambda e: e.copy(abh[:, :], ab[:, :]), m_ab)
        m_abl = dve(lambda e: e.tensor_tensor(abl[:, :], ab[:, :], abh[:, :].bitcast(F32), ALU.subtract), a5)

        def alibi_stores():
            wait("sync", m_abl, m_one)
            for dst, at in ((Akd, 0), (Aqd, NH)):
                j = 0 if at == 0 else 2
                dma("sync", "alibi", dst[:, j, :], abh[at:at + NH, :].bitcast(F32))
                dma("sync", "alibi", dst[:, j + 1, :], abl[at:at + NH, :].bitcast(F32))
                dma("sync", "alibi", dst[:, 2 - j, :], one[0:NH, :])
                last = dma("sync", "alibi", dst[:, 3 - j, :], one[0:NH, :])
            return last

        def wsource(e):
            if e < NE:
                return t["W1"][e], t["W2"][e], t["W3"][e]
            a = (e - NE) * HE
            return t["Ws1"][:, a:a + HE], t["Ws2"][:, a:a + HE], t["Ws3"][a:a + HE, :]

        m_split, m_wstore = {}, {}

        def load_expert(e):
            k = e % 2
            w1, w2, w3 = wsource(e)
            wait("sync", *(m_split.get(e - 2) or (m_wz,)))
            nm = f"wraw{k}"
            dma("sync", nm, wraw[:, k, 0:W2_AT].rearrange("p (c n) -> p c n", c=2), rows(w1))
            dma("sync", nm, wraw[:, k, W2_AT:W3_AT].rearrange("p (c n) -> p c n", c=2), rows(w2))
            dma("sync", nm, wraw[:, k, W3_AT:W3_AT + 2 * D].rearrange("p (c n) -> p c n", c=2), rows(w3[0:2 * P, :]))
            return dma("sync", nm, wraw[0:96, k, W3_AT + 2 * D:RAW], w3[2 * P:HE, :])

        def split_expert(e, loaded):
            k = e % 2
            a = act(lambda q: q.copy(wsp[:, k, 0:RAW], wraw[:, k, :]), loaded, m_wz, m_wstore.get(e - 2))
            b = pool(lambda q: q.tensor_tensor(wsp[:, k, RAW:2 * RAW], wraw[:, k, :],
                                               wsp[:, k, 0:RAW].bitcast(F32), ALU.subtract), a)
            m_split[e] = (a, b)

        def store_expert(e):
            k = e % 2
            m_wstore[e] = dma("sync", f"wst{k}", Wd[e * P:(e + 1) * P, :], wsp[:, k, :].bitcast(F32), *m_split[e])

        x_v = t["x"].rearrange("b s d -> (b s) d").rearrange("(g j p) d -> g p j d", p=P, j=4)
        xn_v = Xn.rearrange("(g j p) d -> g p j d", p=P, j=4)
        v_v = Vd.rearrange("(g j p) n -> g p j n", p=P, j=4)
        m_x, m_norm, m_rstd, m_xnst, m_xev, m_xmm, m_qkst, m_vst, m_tr = {}, {}, {}, {}, {}, {}, {}, {}, {}
        free = {}

        def load_x(g):
            m_x[g] = dma("sync", f"x{g % 3}", xt[:, g % 3, :, :], x_v[g], m_norm.get(g - 3))

        def layer_stats(g):
            k = g % 2
            for j in range(4):
                s = dve(lambda e, j=j: e.bn_stats(stats[:, k, j, :], xt[:, g % 3, j, :]), m_x[g])
            for j in range(4):
                s = dve(lambda e, j=j: e.bn_aggr(mv[:, k, j, :], stats[:, k, j, :]), s if j == 0 else None)
            s = dve(lambda e: e.tensor_scalar(veps[:, k, :], mv[:, k, :, 1], EPS, None, ALU.add), s)
            m_rstd[g] = pool(lambda e: e.tensor_tensor(rstd[:, k, :], veps[:, k, :], nhalf[:, :], ALU.pow), s, m_nhalf)

        def normalise(g):
            k = g % 2
            wait("vector", m_rstd[g], m_tr.get(g - 2), m_xnst.get(g - 2))
            for j in range(4):
                s = dve(lambda e, j=j: e.tensor_scalar(xn[:, k, j, :], xt[:, g % 3, j, :], mv[:, k, j, 0:1],
                                                       rstd[:, k, j:j + 1], ALU.subtract, ALU.mult))
            m_norm[g] = s
            m_xnst[g] = dma("sync", f"xn{k}", xn_v[g], xn[:, k, :, :], s)

        def to_columns(src, banks, hi, lo, *m):
            wait("tensor", m_ident, *m, *free.get(banks[0], ()), *free.get(banks[1], ()))
            for c in range(2):
                for j in range(4):
                    tr = transpose(ps[:, banks[c], j * P:(j + 1) * P], src[:, j, c * P:(c + 1) * P],
                                   sig=c == 1 and j == 3)
            b = banks[0]
            a = act(lambda e: e.copy(hi, ps[:, b:b + 2, :]), tr)
            d = dve(lambda e: e.tensor_tensor(lo, ps[:, b:b + 2, :], hi.bitcast(F32), ALU.subtract), a)
            free[banks[0]] = free[banks[1]] = (a, d)
            return tr, (a, d)

        def columns(g):
            k = g % 2
            b = 2 * k
            wait("scalar", *m_xmm.get(g - 2, ()))
            wait("vector", *m_xmm.get(g - 2, ()))
            m_tr[g], m_xev[g] = to_columns(xn[:, k, :, :], (b, b + 1), XH[:, k, :, :], XL[:, k, :, :], m_norm[g])

        ring_a = [0]

        def project(g):
            k = g % 2
            wait("tensor", *m_xev[g], m_wq, m_wk, m_wv)
            wait("scalar", *m_qkst.get(g - 2, ()), m_bq)
            wait("vector", *m_qkst.get(g - 2, ()), m_vst.get(g - 2), m_vs, m_w)
            for o in range(4):
                bank = 4 + ring_a[0] % 4
                ring_a[0] += 1
                w, m0 = o // 2, (o % 2) * P
                q = mm3(ps[:, bank, :], [(Wqk["h"][:, w, c, m0:m0 + P], Wqk["l"][:, w, c, m0:m0 + P],
                                          XH[:, k, c, :], XL[:, k, c, :]) for c in range(2)],
                        *free.get(bank, ()), sig=True)
                a = act(lambda e, o=o, bank=bank: e.activation(qkH[:, k, o, :], ps[:, bank, :], ACT.Identity,
                                                               bias=bqk[:, o:o + 1]), q)
                d = dve(lambda e, o=o, bank=bank: e.scalar_tensor_tensor(
                    qkL[:, k, o, :], ps[:, bank, :], bqk[:, o:o + 1], qkH[:, k, o, :].bitcast(F32),
                    ALU.add, ALU.subtract), a)
                free[bank] = (a, d)
            at = slice(g * GT, (g + 1) * GT)
            s1 = dma("sync", f"qh{k}", QKh.rearrange("(o p) n -> p o n", p=P)[:, :, at], qkH[:, k, :, :].bitcast(F32), a)
            s2 = dma("sync", f"ql{k}", QKl.rearrange("(o p) n -> p o n", p=P)[:, :, at], qkL[:, k, :, :].bitcast(F32), d)
            m_qkst[g] = (s1, s2)
            for j in range(4):
                bank = 4 + ring_a[0] % 4
                ring_a[0] += 1
                q = mm3(ps[:, bank, 0:D + NE], [(XH[:, k, c, j * P:(j + 1) * P], XL[:, k, c, j * P:(j + 1) * P],
                                                 Wv["h"][:, c, :], Wv["l"][:, c, :]) for c in range(2)],
                        *free.get(bank, ()), sig=True)
                d = dve(lambda e, j=j, bank=bank: e.tensor_tensor(
                    vs[:, k, j, :, 0:HD], ps[:, bank, 0:D].rearrange("p (h d) -> p h d", h=NH),
                    bvr[:, :].rearrange("p (h d) -> p h d", h=NH), ALU.add), q)
                d2 = dve(lambda e, j=j, bank=bank: e.tensor_copy(Lg[:, 4 * g + j, :], ps[:, bank, D:D + NE]))
                free[bank] = (d, d2)
            m_xmm[g] = (q,)
            m_vst[g] = dma("sync", f"vs{k}", v_v[g], vs[:, k, :, :, :].rearrange("p j h d -> p j (h d)"), d)
            return d2

        load_x(0)
        load_x(1)
        m_alibi = alibi_stores()
        layer_stats(0)
        normalise(0)
        columns(0)
        loaded = {0: load_expert(0)}
        for g in range(NG):
            if g + 1 < NG:
                layer_stats(g + 1)
                if g + 2 < NG:
                    load_x(g + 2)
                normalise(g + 1)
                columns(g + 1)
            m_lg = project(g)
            if g < NE + 2:
                split_expert(g, loaded[g])
                if g + 1 < NE + 2:
                    loaded[g + 1] = load_expert(g + 1)
                store_expert(g)
            if g >= 4:
                zs = range((g - 4) * NBLK // 12, (g - 3) * NBLK // 12)
                for b in zs:
                    m_zs = dma("sync", "zero", Xs[b * GT:(b + 1) * GT, :].rearrange("(p j) d -> p (j d)", p=P),
                               zero[:, 0:4 * D], m_zero)
        pr.phase_a_done = [m_lg, m_split[NE + 1][1], m_split[NE + 1][0], *m_qkst[NG - 1], *m_qkst[NG - 2],
                           m_vst[NG - 1], m_vst[NG - 2], m_xnst[NG - 1], m_xnst[NG - 2],
                           m_wstore[NE + 1], m_wstore[NE], m_zs, m_alibi, *m_xmm[NG - 1], m_wo]
        A.close()

        R = ExitStack()
        rt = {n: sbuf(R, "r_" + n, [P, NT, NE]) for n in ("eq", "o1", "o2", "l2", "t", "pa", "pb")}
        rs = {n: sbuf(R, "r_" + n, [P, NT]) for n in ("m1", "m2", "r", "s")}
        cnt = {n: sbuf(R, "r_" + n, [P, NE]) for n in ("nb", "ia", "ib", "base")}
        cmp16 = sbuf(R, "cmp16", [P, NE, 16])
        cmpb = sbuf(R, "cmpb", [P, NBLK, NE])
        bex = sbuf(R, "bex", [P, NBLK])
        tri = sbuf(R, "tri", [P, P])
        onesm = sbuf(R, "onesm", [P, P])
        crow = sbuf(R, "crow", [P, 8 + 16 + NBLK + 1])
        done_a = pr.phase_a_done
        wait("sync", *done_a)
        dma("sync", "c_r", tri[:, :], t["c_tri"])
        m_cr = dma("sync", "c_r", crow[:, :], t["c_row"])
        m_ones = pool(lambda e: e.memset(onesm[:, :], 1.0), *done_a)
        wait("vector", *done_a, m_cr)

        def over_tiles(a):
            return a.rearrange("p (u e) -> p u e", u=1).broadcast_to([P, NT, NE])

        def over_experts(a):
            return a.rearrange("p (n u) -> p n u", u=1).broadcast_to([P, NT, NE])

        rev = over_tiles(crow[:, 0:8])

        def tt(o, a, b, op, *m):
            return dve(lambda e: e.tensor_tensor(o, a, b, op), *m)

        def red(o, a, op, *m):
            return dve(lambda e: e.tensor_reduce(o, a, AX.X, op), *m)

        def first_of(best, one_hot, logits, m):
            m = red(best, logits, ALU.max, m)
            m = tt(rt["eq"][:, :, :], logits, over_experts(best), ALU.is_equal, m)
            m = tt(rt["t"][:, :, :], rt["eq"][:, :, :], rev, ALU.mult, m)
            m = red(rs["r"][:, :], rt["t"][:, :, :], ALU.max, m)
            return tt(one_hot, rt["t"][:, :, :], over_experts(rs["r"][:, :]), ALU.is_equal, m)

        m = first_of(rs["m1"][:, :], rt["o1"][:, :, :], Lg[:, :, :], None)
        m = dve(lambda e: e.scalar_tensor_tensor(rt["l2"][:, :, :], rt["o1"][:, :, :], -3.0e38, Lg[:, :, :],
                                                 ALU.mult, ALU.add), m)
        m = first_of(rs["m2"][:, :], rt["o2"][:, :, :], rt["l2"][:, :, :], m)
        m_d = tt(rs["s"][:, :], rs["m2"][:, :], rs["m1"][:, :], ALU.subtract, m)
        m_e = act(lambda e: e.activation(rs["s"][:, :], rs["s"][:, :], ACT.Exp), m_d)
        m_m = tt(rt["eq"][:, :, :], rt["o1"][:, :, :], rt["o2"][:, :, :], ALU.add, m)
        m = dve(lambda e: e.tensor_scalar(rs["r"][:, :], rs["s"][:, :], 1.0, None, ALU.add), m_e, m_m)
        m = dve(lambda e: e.reciprocal(prob[:, 0, :], rs["r"][:, :]), m)
        m_prob = tt(prob[:, 1, :], rs["s"][:, :], prob[:, 0, :], ALU.mult, m)
        flat = rt["eq"][:, :, :].rearrange("p n e -> p (n e)")
        mm(ps[:, 0, :], tri[:, :], flat, True, True, m_m, m_cr, m_ones, *done_a)
        mr = mm(ps[:, 1, :], onesm[:, :], flat, True, True, sig=True)
        b0 = ps[:, 0, :].rearrange("p (n e) -> p n e", e=NE)
        b1 = ps[:, 1, :].rearrange("p (n e) -> p n e", e=NE)
        m = dve(lambda e: e.tensor_copy(rt["pa"][:, :, :], b1), mr)
        a, b = rt["pa"], rt["pb"]
        sh = 1
        while sh < NT:
            m = dve(lambda e, a=a, b=b, sh=sh: e.tensor_copy(b[:, 0:sh, :], a[:, 0:sh, :]), m)
            m = tt(b[:, sh:NT, :], a[:, sh:NT, :], a[:, 0:NT - sh, :], ALU.add, m)
            a, b = b, a
            sh *= 2
        total = a[:, NT - 1, :]
        m2 = tt(cmp16[:, :, :], total.rearrange("p (e u) -> p e u", u=1).broadcast_to([P, NE, 16]),
                crow[:, 8:24].rearrange("p (u j) -> p u j", u=1).broadcast_to([P, NE, 16]), ALU.is_gt, m)
        m2 = red(cnt["nb"][:, :], cmp16[:, :, :], ALU.add, m2)
        ia, ib = cnt["ia"], cnt["ib"]
        m2 = dve(lambda e: e.tensor_copy(cnt["ia"][:, :], cnt["nb"][:, :]), m2)
        sh = 1
        while sh < NE:
            m2 = dve(lambda e, ia=ia, ib=ib, sh=sh: e.tensor_copy(ib[:, 0:sh], ia[:, 0:sh]), m2)
            m2 = tt(ib[:, sh:NE], ia[:, sh:NE], ia[:, 0:NE - sh], ALU.add, m2)
            ia, ib = ib, ia
            sh *= 2
        m3 = tt(cnt["base"][:, :], ia[:, :], cnt["nb"][:, :], ALU.subtract, m2)
        m4 = tt(cmpb[:, :, :], crow[:, 24:24 + NBLK].rearrange("p (b u) -> p b u", u=1).broadcast_to([P, NBLK, NE]),
                ia[:, :].rearrange("p (u e) -> p u e", u=1).broadcast_to([P, NBLK, NE]), ALU.is_ge, m3)
        m4 = red(bex[:, :], cmpb[:, :, :], ALU.add, m4)
        m4 = dve(lambda e: e.tensor_scalar(bex[:, :], bex[:, :], float(NE - 1), float(P), ALU.min, ALU.mult), m4)
        m_widx = dve(lambda e: e.tensor_scalar(widx[:, :], bex[:, :], crow[:, 24 + NBLK:25 + NBLK], None, ALU.add), m4)
        m = tt(b[:, :, :], a[:, :, :], b1, ALU.subtract, m4)
        m = tt(b[:, :, :], b[:, :, :], b0, ALU.add, m)
        m = dve(lambda e, b=b: e.scalar_tensor_tensor(b[:, :, :], over_tiles(cnt["base"][:, :]), float(GT), b[:, :, :],
                                                      ALU.mult, ALU.add), m)
        m = tt(rt["t"][:, :, :], b[:, :, :], rt["o1"][:, :, :], ALU.mult, m)
        m = red(rs["m1"][:, :], rt["t"][:, :, :], ALU.add, m)
        m = dve(lambda e: e.tensor_copy(slot[:, 0, :], rs["m1"][:, :]), m)
        m = tt(rt["t"][:, :, :], b[:, :, :], rt["o2"][:, :, :], ALU.mult, m)
        m = red(rs["m2"][:, :], rt["t"][:, :, :], ALU.add, m)
        m_slot = dve(lambda e: e.tensor_copy(slot[:, 1, :], rs["m2"][:, :]), m)
        R.close()

        def scatter_tokens():
            last = [None, None]
            for g in range(NG):
                k = g % 2
                ld = dma("gpsimd", f"xg{k}", xg[:, k, :, :], xn_v[g], last[k], *done_a)
                wait("gpsimd", ld, m_slot)
                for j in range(4):
                    for c in range(2):
                        nm = f"sc{k}"
                        s = pr.sem(nm)
                        pr.at[nm] += 16
                        pr.queues["gpsimd"].append(
                            lambda e, j=j, c=c, s=s, i=4 * g + j, k=k: e.indirect_dma_start(
                                Xs[:, :], bass.IndirectOffsetOnAxis(ap=slot[:, c, i:i + 1], axis=0),
                                xg[:, k, j, :], None).then_inc(s, 16))
                last[k] = (nm, pr.at[nm])
            return last

        m_scat = scatter_tokens()

        B = ExitStack()
        QO = sbuf(B, "QO", [P, 3, 2, S], F32R)
        KO = sbuf(B, "KO", [P, 3, 2, S], F32R)
        NP_ = 10
        pt = sbuf(B, "pt", [P, NP_, S])
        vb = sbuf(B, "vb", [P, 2, 8, NH * 32])
        mx = sbuf(B, "mx", [P, 2, 2, 8, 2])
        m16 = sbuf(B, "m16", [P, 2, 2, 8])
        mneg = sbuf(B, "mneg", [P, 2, 2, 2, 8])
        mT = sbuf(B, "mT", [32, 2, P], F32R)
        accs = sbuf(B, "accs", [P, 2, GT])
        rc = sbuf(B, "rc", [P, 2, 4, 4])
        ot = sbuf(B, "ot", [P, 2, 8, D])
        NPAIR = NB * NH // 2

        wait("gpsimd", m_slot)
        mz = None
        ordered = []
        for tns in (QO, KO):
            for rows_ in (slice(64, 96), slice(96, 128)):
                mz = dve(lambda e, tns=tns, rows_=rows_: e.memset(tns[rows_, :, :, :].bitcast(F32), 0.0), *done_a, m_slot)
        m_opz = dve(lambda e: e.memset(KO[96:98, :, :, :].bitcast(F32), 1.0), mz)

        m_ops, m_st_last, m_a_last, m_mrow = {}, {}, {}, {}

        def load_pair(r):
            b, j = divmod(r, NH // 2)
            k = r % 3
            wait("sync", m_opz, m_st_last.get(r - 3), m_a_last.get(r - 3), *done_a)
            nm = f"op{k}"
            at = slice(b * S, (b + 1) * S)
            for dst, o, parts, al in ((QO, 0, (QKh, QKl, QKh, QKl), Aqd), (KO, D, (QKh, QKh, QKl, QKl), Akd)):
                for i, src in enumerate(parts):
                    r0 = o + 32 * j
                    dma("sync", nm, dst[16 * i:16 * i + 16, k, :, :].bitcast(F32),
                        src[r0:r0 + 32, at].rearrange("(h d) n -> d h n", d=HD))
                last = dma("sync", nm, dst[64:68, k, :, :].bitcast(F32),
                           al[2 * j:2 * j + 2, :, :].rearrange("h r n -> r h n"))
            m_ops[r] = last

        m_v, m_pv_batch = {}, {}

        def load_v(b):
            m_v[b] = dma("sync", f"vb{b % 2}", vb[:, b % 2, :, :],
                         Vd.rearrange("(b c p) n -> b p c n", p=P, c=8)[b], m_pv_batch.get(b - 2), *done_a)

        for b in range(8):
            free[b] = tuple(done_a) + (m_slot,)
        px = [0]

        def take():
            bank = 5 + px[0] % 3
            px[0] += 1
            return bank

        m_mxfree = {}

        def score_max(r, u):
            hh, i, half = u // 16, (u // 2) % 8, u % 2
            k = r % 3
            bank = take()
            q = mm(ps[:, bank, :], QO[0:96, k, hh, i * P:(i + 1) * P], KO[0:96, k, hh, half * GT:(half + 1) * GT],
                   True, True, m_ops[r], *free[bank], sig=True)
            d = dve(lambda e: e.reduce_max(mx[:, r % 2, hh, i, half:half + 1], ps[:, bank, :], AX.X), q)
            free[bank] = (d,)
            if u == 31:
                m_a_last[r] = q
                k2 = r % 2
                m = dve(lambda e: e.tensor_reduce(m16[:, k2, :, :], mx[:, k2, :, :, :], AX.X, ALU.max), d)
                m1 = dve(lambda e: e.tensor_scalar(mneg[:, k2, :, 0, :].bitcast(F32R), m16[:, k2, :, :], -1.0, None,
                                                   ALU.mult), m, m_mxfree.get(r - 2))
                m_mrow[r] = dve(lambda e: e.scalar_tensor_tensor(mneg[:, k2, :, 1, :], m16[:, k2, :, :], -1.0,
                                                                 mneg[:, k2, :, 0, :], ALU.mult, ALU.subtract), m1)

        m_max = {}

        def max_rows(r):
            k2 = r % 2
            bank = take()
            q = transpose(ps[0:32, bank, 0:P], mneg[:, k2, :, :, :].rearrange("p h l i -> p (h l i)"),
                          m_mrow[r], m_ident, *free[bank], sig=True)
            m_mxfree[r] = q
            d = dve(lambda e: e.tensor_copy(mT[:, k2, :], ps[0:32, bank, 0:P]), q, m_max.get(r - 2))
            free[bank] = (d,)
            for hh in range(2):
                m_max[r] = dma("sync", f"mx{k2}", QO[96:98, r % 3, hh, :].bitcast(F32).rearrange("l (i n) -> l i n", n=P),
                               mT[16 * hh:16 * hh + 16, k2, :].bitcast(F32), d)

        m_exp, m_pv, m_pfree, m_acc = {}, {}, {}, {}
        n_exp = [0]
        p_of = {}

        def scores_exp(r, kc, hh):
            k = r % 3
            n = n_exp[0]
            n_exp[0] += 1
            b0_ = 2 * (n % 2)
            wait("tensor", m_ops[r], m_max[r], *free[b0_], *free[b0_ + 1])
            for half in range(2):
                q = mm(ps[:, b0_ + half, :], KO[:, k, hh, kc * P:(kc + 1) * P], QO[:, k, hh, half * GT:(half + 1) * GT],
                       True, True, sig=half == 1)
            if kc == 7 and hh == 1:
                m_st_last[r] = q
            s = n % NP_
            p_of[r, kc, hh] = s
            a = act(lambda e: e.activation(pt[:, s, :], ps[:, b0_:b0_ + 2, :], ACT.Exp), q, m_pfree.get(s))
            free[b0_] = free[b0_ + 1] = (a,)
            m_exp[r, kc, hh] = a

        def values(r, kc):
            b, j = divmod(r, NH // 2)
            wait("tensor", m_exp[r, kc, 0], m_exp[r, kc, 1], m_v[b], *(free[4] if kc == 0 else ()))
            for hh in range(2):
                for half in range(2):
                    g4 = 2 * hh + half
                    q = mm(ps[32 * g4:32 * g4 + 32, 4, :], vb[:, b % 2, kc, 32 * (2 * j + hh):32 * (2 * j + hh) + 32],
                           pt[:, p_of[r, kc, hh], half * GT:(half + 1) * GT], kc == 0, kc == 7, sig=g4 == 3)
            for hh in range(2):
                m_pfree[p_of[r, kc, hh]] = q
            if kc == 7:
                m_pv_batch[b] = q
                k2 = r % 2
                a = act(lambda e: e.copy(accs[:, k2, :], ps[:, 4, :]), q, m_acc.get(r - 2))
                free[4] = (a,)
                m_pv[r] = a

        m_ot, m_od = {}, {}

        def normalise_heads(r):
            b, j = divmod(r, NH // 2)
            k2 = r % 2
            bank = take()
            wait("tensor", m_pv[r], *free[bank])
            for c in range(4):
                q = transpose(ps[:, bank, c * P:(c + 1) * P], accs[:, k2, c * P:(c + 1) * P], sig=c == 3)
            m_acc[r] = q
            v = ps[:, bank, :].rearrange("p (c g d) -> p c g d", c=4, g=4)
            m = dve(lambda e: e.reciprocal(rc[:, k2, :, :], v[:, :, :, HD]), q)
            wait("vector", m, m_od.get(b - 2))
            for hh in range(2):
                h = 2 * j + hh
                o = ot[:, b % 2, :, HD * h:HD * h + HD].rearrange("p (f c) d -> p c f d", f=2)
                m = dve(lambda e, hh=hh, o=o: e.tensor_tensor(
                    o, v[:, :, 2 * hh:2 * hh + 2, 0:HD],
                    rc[:, k2, :, 2 * hh:2 * hh + 2].rearrange("p c (g u) -> p c g u", u=1).broadcast_to([P, 4, 2, HD]),
                    ALU.mult))
            free[bank] = (m,)
            if j == NH // 2 - 1:
                m_od[b] = dma("sync", f"od{b % 2}", Od.rearrange("(b c p) d -> b p c d", p=P, c=8)[b],
                              ot[:, b % 2, :, :], m)

        load_pair(0)
        load_v(0)
        load_pair(1)
        load_v(1)
        AHEAD = 12
        step_of_a = [0]

        def max_step():
            s = step_of_a[0]
            step_of_a[0] += 1
            if s >= 8 * NPAIR:
                return [lambda: None] * 4
            r, w = divmod(s, 8)
            return [lambda u=4 * w + i: score_max(r, u) for i in range(4)]

        for s in range(AHEAD):
            if s == 8:
                load_pair(2)
            if s == 9:
                max_rows(0)
            for f in max_step():
                f()
        LAG = 2
        todo = []
        for s in range(8 * NPAIR + LAG + 1):
            r, kc = divmod(s, 8)
            units = max_step()
            if r < NPAIR:
                scores_exp(r, kc, 0)
            units[0]()
            if r < NPAIR:
                scores_exp(r, kc, 1)
            units[1]()
            units[2]()
            if LAG <= s < 8 * NPAIR + LAG:
                values(*divmod(s - LAG, 8))
            units[3]()
            if s >= LAG + 8 and (s - LAG) % 8 == 0:
                normalise_heads((s - LAG) // 8 - 1)
            if kc == 5 and r + 1 < NPAIR:
                max_rows(r + 1)
            if kc == 0 and r >= 1 and r + 2 < NPAIR:
                load_pair(r + 2)
            if kc == 4 and r % 8 == 0 and 8 <= r < NPAIR - 8:
                load_v(r // 8 + 1)
        done_b = [m_od[NB - 1], m_od[NB - 2], m_pv[NPAIR - 1], m_acc[NPAIR - 1], m_st_last[NPAIR - 1], m_a_last[NPAIR - 1],
                  free[5][0], free[6][0], free[7][0], *free[0], *free[2], m_max[NPAIR - 1], m_v[NB - 1]]
        B.close()

        C = ExitStack()
        wb = sbuf(C, "wb", [P, 3, 2 * RAW], F32R)
        xr = sbuf(C, "xr", [P, 2, 4, D])
        orow = sbuf(C, "orow", [P, 1, 4, D])
        CH, CL = (sbuf(C, n, [P, 2, 2, GT], F32R) for n in ("CH", "CL"))
        OH, OL = (sbuf(C, n, [P, 1, 2, GT], F32R) for n in ("OH", "OL"))
        sg = sbuf(C, "sg", [P, 2, GT])
        hf = sbuf(C, "hf", [P, 2, GT])
        HH, HL = (sbuf(C, n, [P, 8, GT], F32R) for n in ("HH", "HL"))
        yT = sbuf(C, "yT", [P, 2, GT])
        yr = sbuf(C, "yr", [P, 2, 4, D])
        gath = sbuf(C, "gath", [P, 4, 2, D])
        xres = sbuf(C, "xres", [P, 4, D])
        for e_ in ("scalar", "vector", "tensor", "sync", "gpsimd"):
            wait(e_, *done_b)
        for b in range(8):
            free[b] = ()
        gu = [0]
        nh = [0]
        m_wb, m_wbfree, m_xr, m_xcol, m_xused, m_xrfree = {}, {}, {}, {}, {}, {}
        m_h, m_hfree, m_sg, m_hf = {}, {}, {}, {}

        def gate_up(xh, xl, w, hc, *m):
            h0, hn = HC[hc]
            n = nh[0]
            nh[0] += 1
            s, k = n % 8, n % 2
            banks = (2 + 2 * (n % 2), 3 + 2 * (n % 2))
            wait("tensor", *m)
            for which, bank in zip((0, W2_AT), banks):
                ks = []
                for c in range(2):
                    a = which + c * HE + h0
                    ks.append((w[:, a:a + hn], w[:, RAW + a:RAW + a + hn], xh[:, c, :], xl[:, c, :]))
                q = mm3(ps[0:hn, bank, :], ks, *free[bank], sig=True)
                if which == 0:
                    a_ = act(lambda e: e.activation(sg[0:hn, k, :], ps[0:hn, banks[0], :], ACT.Silu), q, m_hf.get(n - 2))
                    free[banks[0]] = (a_,)
            d = dve(lambda e: e.tensor_tensor(hf[0:hn, k, :], ps[0:hn, banks[1], :], sg[0:hn, k, :], ALU.mult),
                    q, a_, *m_h.get(n - 2, ()))
            free[banks[1]] = (d,)
            m_hf[n] = d
            a2 = act(lambda e: e.copy(HH[0:hn, s, :], hf[0:hn, k, :]), d, m_hfree.get(s))
            d2 = dve(lambda e: e.tensor_tensor(HL[0:hn, s, :], hf[0:hn, k, :], HH[0:hn, s, :].bitcast(F32),
                                               ALU.subtract), a2)
            m_h[n] = (a2, d2)
            return n

        def down(chunks, extra=()):
            for mc in range(2):
                ks = []
                for w, hc, n in chunks:
                    hn = HC[hc][1]
                    a = W3_AT + hc * D + mc * P
                    wait("tensor", *m_h[n])
                    ks.append((w[0:hn, a:a + P], w[0:hn, RAW + a:RAW + a + P], HH[0:hn, n % 8, :], HL[0:hn, n % 8, :]))
                for wh, wl, xh, xl in extra:
                    ks.append((wh[:, mc * P:(mc + 1) * P], wl[:, mc * P:(mc + 1) * P], xh, xl))
                q = mm3(ps[:, 6 + mc, :], ks, *free[6 + mc], sig=True)
            for _, _, n in chunks:
                m_hfree[n % 8] = q
            return q

        m_yT, m_yTfree, m_yr = {}, {}, {}

        def rows_back(*m):
            wait("tensor", *m, *free[0], *free[1])
            for j in range(4):
                for mc in range(2):
                    q = transpose(ps[:, j // 2, (j % 2) * D + mc * P:(j % 2) * D + (mc + 1) * P],
                                  yT[:, mc, j * P:(j + 1) * P], sig=j == 3 and mc == 1)
            return q

        xs_v = Xs.rearrange("(b j p) d -> b p j d", p=P, j=4)
        ys_v = Ys.rearrange("(b j p) d -> b p j d", p=P, j=4)

        def gather_weights(b):
            k = b % 3
            wait("gpsimd", m_widx, m_wbfree.get(b - 3))
            nm = f"wb{k}"
            s = pr.sem(nm)
            pr.at[nm] += 16
            pr.queues["gpsimd"].append(lambda e: e.indirect_dma_start(
                wb[:, k, :].bitcast(F32), None, Wd[:, :],
                bass.IndirectOffsetOnAxis(ap=widx[:, b:b + 1], axis=0)).then_inc(s, 16))
            m_wb[b] = (nm, pr.at[nm])

        def load_slots(b):
            m_xr[b] = dma("sync", f"xr{b % 2}", xr[:, b % 2, :, :], xs_v[b], m_xrfree.get(b - 2), *m_scat, m_zs)

        def slot_columns(b):
            k = b % 2
            wait("scalar", m_xused.get(b - 2))
            wait("vector", m_xused.get(b - 2))
            m_xrfree[b], m_xcol[b] = to_columns(xr[:, k, :, :], (0, 1), CH[:, k, :, :], CL[:, k, :, :], m_xr[b])

        h_of = {}

        def block_up(b, hc):
            k = b % 2
            h_of[b, hc] = gate_up(CH[:, k, :, :], CL[:, k, :, :], wb[:, b % 3, :], hc, *m_xcol[b], m_wb[b])
            m_xused[b] = ("tensor", pr.at["tensor"])

        last_yT = [None]

        def block_down(b):
            q = down([(wb[:, b % 3, :], hc, h_of[b, hc]) for hc in range(3)])
            m_wbfree[b] = q
            a = act(lambda e: e.copy(yT[:, :, :], ps[:, 6:8, :]), q, last_yT[0])
            free[6] = free[7] = (a,)
            m_yT[b] = a

        def block_out(b):
            q = rows_back(m_yT[b])
            last_yT[0] = q
            k = b % 2
            d = dve(lambda e: e.tensor_copy(yr[:, k, :, :].rearrange("p j d -> p (j d)"),
                                            ps[:, 0:2, :].rearrange("p a n -> p (a n)")), q, m_yr.get(b - 2))
            free[0] = free[1] = (d,)
            m_yr[b] = dma("sync", f"yr{k}", ys_v[b], yr[:, k, :, :], d)

        gather_weights(0)
        gather_weights(1)
        load_slots(0)
        load_slots(1)
        slot_columns(0)
        for b in range(NBLK + 1):
            if b < NBLK:
                block_up(b, 0)
            if b >= 1:
                block_down(b - 1)
            if b < NBLK:
                block_up(b, 1)
                if b + 1 < NBLK:
                    slot_columns(b + 1)
                block_up(b, 2)
            if b >= 1:
                block_out(b - 1)
            if b + 2 < NBLK:
                gather_weights(b + 2)
                load_slots(b + 2)

        done_c = [m_yr[NBLK - 1], m_yr[NBLK - 2]]
        ms = {}
        for i in range(2):
            ms[i] = dma("sync", f"ws{i}", wb[:, i, :].bitcast(F32), Wd[(NE + i) * P:(NE + i + 1) * P, :],
                        m_wbfree[NBLK - 1], m_wbfree[NBLK - 2], m_wbfree[NBLK - 3])
        od_v = Od.rearrange("(g j p) d -> g p j d", p=P, j=4)
        out_v = out.rearrange("b s d -> (b s) d").rearrange("(g j p) d -> g p j d", p=P, j=4)
        m_xr2, m_or, m_orfree, m_oc, m_gf, m_g, m_res, m_resf = {}, {}, {}, {}, {}, {}, {}, {}
        base = NBLK

        def load_rows(g):
            k = (base + g) % 2
            m_xr[base + g] = dma("sync", f"xr{k}", xr[:, k, :, :], xn_v[g], m_xrfree.get(base + g - 2))

        def load_o(g):
            m_or[g] = dma("sync", "or", orow[:, 0, :, :], od_v[g], m_orfree.get(g - 1))

        def o_columns(g):
            wait("scalar", m_xused.get(base + g - 1))
            wait("vector", m_xused.get(base + g - 1), )
            wait("scalar", m_ydone.get(g - 1))
            wait("vector", m_ydone.get(g - 1))
            m_orfree[g], m_oc[g] = to_columns(orow[:, 0, :, :], (0, 1), OH[:, 0, :, :], OL[:, 0, :, :], m_or[g])

        m_ydone = {}
        m_out = {}

        def gather_rows(g, j):
            i = 4 * g + j
            wait("gpsimd", *done_c, m_gf.get(i - 4), m_prob)
            nm = f"ga{j}"
            for c in range(2):
                s = pr.sem(nm)
                pr.at[nm] += 16
                pr.queues["gpsimd"].append(lambda e, c=c, s=s: e.indirect_dma_start(
                    gath[:, j, c, :], None, Ys[:, :],
                    bass.IndirectOffsetOnAxis(ap=slot[:, c, i:i + 1], axis=0)).then_inc(s, 16))
            m_g[i] = (nm, pr.at[nm])

        def load_res(g):
            m_res[g] = dma("sync", "res", xres[:, :, :], x_v[g], m_resf.get(g - 1))

        def shared_up(g, e, hc):
            k = (base + g) % 2
            h_of[base + g, e, hc] = gate_up(CH[:, k, :, :], CL[:, k, :, :], wb[:, e, :], hc, *m_xcol[base + g], ms[e])
            m_xused[base + g] = ("tensor", pr.at["tensor"])

        def shared_down(g):
            q = down([(wb[:, e, :], hc, h_of[base + g, e, hc]) for e in range(2) for hc in range(3)],
                     [(WoH[:, c, :], WoL[:, c, :], OH[:, 0, c, :], OL[:, 0, c, :]) for c in range(2)])
            m_ydone[g] = q
            wait("scalar", last_yT[0], m_boc, q)
            for mc in range(2):
                a = act(lambda e, mc=mc: e.activation(yT[:, mc, :], ps[:, 6 + mc, :], ACT.Identity,
                                                      bias=boc[:, mc:mc + 1]))
            free[6] = free[7] = (a,)
            m_yT[base + g] = a

        def shared_out(g):
            q = rows_back(m_yT[base + g])
            last_yT[0] = q
            k = g % 2
            y = lambda j: ps[:, j // 2, (j % 2) * D:(j % 2) * D + D]
            wait("vector", q, m_yr.get(base + g - 2), m_prob)
            ms1 = []
            for j in range(4):
                i = 4 * g + j
                ms1.append(dve(lambda e, j=j, i=i: e.scalar_tensor_tensor(
                    yr[:, k, j, :], gath[:, j, 0, :], prob[:, 0, i:i + 1], y(j), ALU.mult, ALU.add), m_g[i]))
            free[0] = free[1] = (ms1[3],)
            ms2 = []
            for j in range(4):
                i = 4 * g + j
                ms2.append(dve(lambda e, j=j, i=i: e.scalar_tensor_tensor(
                    yr[:, k, j, :], gath[:, j, 1, :], prob[:, 1, i:i + 1], yr[:, k, j, :], ALU.mult, ALU.add), ms1[j]))
                m_gf[i] = ms2[j]
            a = pool(lambda e: e.tensor_tensor(yr[:, k, :, :], yr[:, k, :, :], xres[:, :, :], ALU.add),
                     ms2[3], m_res[g])
            m_resf[g] = a
            m_yr[base + g] = m_out[g] = dma("sync", f"yr{k}", out_v[g], yr[:, k, :, :], a)

        m_yr[base - 2], m_yr[base - 1] = m_yr[NBLK - 2], m_yr[NBLK - 1]
        load_rows(0)
        load_rows(1)
        load_o(0)
        load_res(0)
        for j in range(4):
            gather_rows(0, j)
        slot_columns(base)
        for g in range(NG + 1):
            if g < NG:
                shared_up(g, 0, 0)
            if g >= 1:
                shared_down(g - 1)
            if g < NG:
                shared_up(g, 0, 1)
                o_columns(g)
                shared_up(g, 0, 2)
            if g >= 1:
                shared_out(g - 1)
                if g < NG:
                    load_res(g)
                    for j in range(4):
                        gather_rows(g, j)
            if g < NG:
                if g + 1 < NG:
                    load_o(g + 1)
                shared_up(g, 1, 0)
                if g + 1 < NG:
                    slot_columns(base + g + 1)
                shared_up(g, 1, 1)
                shared_up(g, 1, 2)
                if g + 2 < NG:
                    load_rows(g + 2)
        wait("sync", m_out[NG - 1], m_out[NG - 2])
        C.close()
        block = ctx.enter_context(nc.Block())
        pr.emit(block)


def constants():
    slopes = (1.0 / 2.0 ** (np.arange(NH, dtype=np.float32) / NH)).astype(np.float32)
    k = np.arange(S, dtype=np.float32) - (S - 1)
    alibi = np.concatenate([slopes[:, None] * k[None, :], slopes[:, None] * -k[None, :]]).astype(np.float32)
    tri = np.triu(np.ones((P, P), np.float32), 1)
    row = np.concatenate([8.0 - np.arange(8), 512.0 * np.arange(16), np.arange(NBLK), [0.0]]).astype(np.float32)
    row = np.tile(row[None, :], (P, 1))
    row[:, -1] = np.arange(P)
    return {"c_ident": np.eye(P, dtype=np.float32), "c_alibi": alibi, "c_tri": tri, "c_row": row}


_NAMES = {"L0_attn_x": "x", "L0_attn_Wq": "Wq", "L0_attn_bq": "bq", "L0_attn_Wk": "Wk", "L0_attn_bk": "bk",
          "L0_attn_Wv": "Wv", "L0_attn_bv": "bv", "L0_attn_Wo": "Wo", "L0_attn_bo": "bo", "L0_ffn_Wg": "Wg",
          "L0_ffn_W1": "W1", "L0_ffn_W2": "W2", "L0_ffn_W3": "W3", "L0_ffn_Ws1": "Ws1", "L0_ffn_Ws2": "Ws2",
          "L0_ffn_Ws3": "Ws3"}


def kernel(**inputs):
    import concourse.bacc as _bacc
    from concourse.bass_utils import run_bass_kernel_spmd as _run

    nc = _bacc.Bacc("TRN2", target_bir_lowering=False, num_devices=1)
    arrays, t = {}, {}
    named = {short: np.ascontiguousarray(inputs[name]) for name, short in _NAMES.items()}
    named.update(constants())
    for short, a in named.items():
        arrays[f"in_{short}"] = a
        t[short] = nc.dram_tensor(f"in_{short}", a.shape, mybir.dt.from_np(a.dtype), kind="ExternalInput").ap()
    out = nc.dram_tensor("out_0", (NB, S, D), F32, kind="ExternalOutput").ap()
    build(nc, t, out)
    r = _run(nc, [arrays], core_ids=[0])
    return r.results[0]["out_0"]
```

```python
from contextlib import ExitStack

import numpy as np

import concourse.bass as bass
from concourse import mybir

F32 = mybir.dt.float32
F32R = mybir.dt.float32r
I32 = mybir.dt.int32
U32 = mybir.dt.uint32
ALU = mybir.AluOpType
ACT = mybir.ActivationFunctionType
AX = mybir.AxisListType

P = 128
NB, S, D = 8, 1024, 256
N = NB * S
NH, HD = 16, 16
NE, HE = 8, 352
HC = ((0, 128), (128, 128), (256, 96))
GT = 512
NG = N // GT
NT = N // P
NBLK = (2 * N - NE) // GT + NE
NSLOT = NBLK * GT
RAW = 4 * HE + 3 * D
W2_AT, W3_AT = 2 * HE, 4 * HE
SCALE = float(HD) ** -0.5
EPS = 1e-5


class Program:

    def __init__(self, nc, ctx):
        self.nc, self.ctx = nc, ctx
        self.queues = {e: [] for e in ("tensor", "vector", "scalar", "gpsimd", "sync")}
        self.sems, self.at, self.waited = {}, {}, {}

    def sem(self, name):
        if name not in self.sems:
            self.sems[name] = self.ctx.enter_context(self.nc.semaphore("s_" + name))
            self.at[name] = 0
        return self.sems[name]

    def wait(self, eng, *marks):
        for m in marks:
            if m is None:
                continue
            name, value = m
            if self.waited.get((eng, name), 0) < value:
                self.waited[eng, name] = value
                self.queues[eng].append(lambda e, s=self.sems[name], v=value: e.wait_ge(s, v))

    def put(self, eng, fn, *marks, sig=True):
        self.wait(eng, *marks)
        if not sig:
            self.queues[eng].append(fn)
            return None
        s = self.sem(eng)
        self.at[eng] += 1
        self.queues[eng].append(lambda e: fn(e).then_inc(s, 1))
        return eng, self.at[eng]

    def dma(self, eng, slot, out, in_, *marks, slow=False):
        self.wait(eng, *marks)
        s = self.sem(slot)
        self.at[slot] += 16
        self.queues[eng].append(
            lambda e: e.dma_start(out, in_, allow_slow_non_contiguous=slow).then_inc(s, 16))
        return slot, self.at[slot]

    def emit(self, block):
        for name, queue in self.queues.items():
            def run(e, queue=queue):
                for fn in queue:
                    fn(e)
            blocks = {"tensor": block.tensor, "vector": block.vector, "scalar": block.scalar,
                            "gpsimd": block.gpsimd, "sync": block.sync}
            blocks[name](run)


def build(nc, t, out):
    ctx = ExitStack()
    with ctx:
        pr = Program(nc, ctx)
        put, dma, wait = pr.put, pr.dma, pr.wait
        pe = lambda fn, *m, sig=False: put("tensor", fn, *m, sig=sig)
        dve = lambda fn, *m: put("vector", fn, *m)
        act = lambda fn, *m: put("scalar", fn, *m)
        pool = lambda fn, *m: put("gpsimd", fn, *m)

        def sbuf(stack, name, shape, dt=F32):
            return stack.enter_context(nc.sbuf_tensor(name, shape, dt))

        def dram(name, shape):
            return nc.dram_tensor(name, shape, F32).ap()

        ps = ctx.enter_context(nc.psum_tensor("ps", [P, 8, 512], F32))

        Xn = dram("Xn", [N, D])
        QKh = dram("QKh", [2 * D, N])
        QKl = dram("QKl", [2 * D, N])
        Vd = dram("Vd", [N, D])
        Alid = dram("Alid", [2, NH, 2, S])
        Wd = dram("Wd", [(NE + 2) * P, 2 * RAW])
        Xs = dram("Xs", [NSLOT, D])
        Ys = dram("Ys", [NSLOT, D])
        Od = dram("Od", [N, D])

        def mm(o, l, r, start, stop, *m, sig=False):
            return pe(lambda e: e.matmul(o, l, r, start=start, stop=stop), *m, sig=sig)

        def mm3(o, ks, *m, sig=False, first=True, last=True):
            wait("tensor", *m)
            n = 3 * len(ks)
            i = 0
            for lh, ll, rh, rl in ks:
                for l, r in ((ll, rh), (lh, rl), (lh, rh)):
                    end = i == n - 1
                    mark = mm(o, l, r, first and i == 0, last and end, sig=sig and end)
                    i += 1
            return mark

        def transpose(o, in_, *m, sig=False):
            return pe(lambda e: e.transpose(o, in_, ident[:, :]), *m, sig=sig)

        ident = sbuf(ctx, "ident", [P, P])
        WoH, WoL = (sbuf(ctx, n, [P, 2, D], F32R) for n in ("WoH", "WoL"))
        bor = sbuf(ctx, "bor", [P, D])
        Lg = sbuf(ctx, "Lg", [P, NT, NE])
        prob = sbuf(ctx, "prob", [P, 2, NT])
        slot = sbuf(ctx, "slot", [P, 2, NT], I32)
        widx = sbuf(ctx, "widx", [P, NBLK], I32)
        vst = sbuf(ctx, "vst", [P, 4, D])
        mx = sbuf(ctx, "mx", [P, 2, 2, 8, 2])
        m16 = sbuf(ctx, "m16", [P, 2, 2, 8])
        mneg = sbuf(ctx, "mneg", [P, 2, 2, 2, 8])
        mT = sbuf(ctx, "mT", [32, 2, P], F32R)
        xr = sbuf(ctx, "xr", [P, 2, 4, D])
        OPS = sbuf(ctx, "OPS", [P, 12 * S], F32R)
        QO = OPS[:, 0:6 * S].rearrange("p (k h n) -> p k h n", k=3, h=2)
        KO = OPS[:, 6 * S:12 * S].rearrange("p (k h n) -> p k h n", k=3, h=2)
        VB = sbuf(ctx, "VB", [P, 8 * S])
        vb = VB[:, :].rearrange("p (b c n) -> p b c n", b=2, c=8)

        m_ident = dma("sync", "c_ident", ident[:, :], t["c_ident"])
        m_bor = dma("sync", "c_bor", bor[:, :], t["bo"].rearrange("(a n) -> a n", a=1).broadcast_to([P, D]))

        A = ExitStack()
        Wst = sbuf(A, "Wst", [P, 2, 2, D])
        Wqk = {k: sbuf(A, "W" + k, [P, 2, 2, D], F32R) for k in ("h", "l")}
        Wvst = sbuf(A, "Wvst", [P, 2, D + NE])
        Wv = {k: sbuf(A, "Wv" + k, [P, 2, D + NE], F32R) for k in ("h", "l")}
        bqk = sbuf(A, "bqk", [P, 4])
        bvr = sbuf(A, "bvr", [P, D])
        nhalf = sbuf(A, "nhalf", [P, 4])
        xt = sbuf(A, "xt", [P, 4, 4, D])
        stats = sbuf(A, "stats", [P, 2, 4, 6])
        mv = sbuf(A, "mv", [P, 2, 4, 2])
        veps = sbuf(A, "veps", [P, 2, 4])
        rstd = sbuf(A, "rstd", [P, 2, 4])
        xn = sbuf(A, "xn", [P, 3, 4, D])
        XH, XL = (sbuf(A, n, [P, 2, 2, GT], F32R) for n in ("XH", "XL"))
        qkH, qkL = (sbuf(A, n, [P, 2, 4, GT], F32R) for n in ("qkH", "qkL"))
        vs = sbuf(A, "vs", [P, 2, 4, D + NE])
        Wost = vs[:, 1, 0:2, 0:D]

        def rows(w):
            return w.rearrange("(c p) n -> p c n", p=P)

        x_v = t["x"].rearrange("b s d -> (b s) d").rearrange("(g j p) d -> g p j d", p=P, j=4)
        m_x, m_norm = {}, {}

        def load_x(g):
            m_x[g] = dma("sync", f"x{g % 4}", xt[:, g % 4, :, :], x_v[g], m_norm.get(g - 4))

        load_x(0)
        dma("sync", "c_w", Wst[:, 0, :, :], rows(t["Wq"]))
        dma("sync", "c_w", Wst[:, 1, :, :], rows(t["Wk"]))
        dma("sync", "c_w", Wvst[:, :, 0:D], rows(t["Wv"]))
        dma("sync", "c_w", Wvst[:, :, D:D + NE], rows(t["Wg"]))
        dma("sync", "c_w", Wost, rows(t["Wo"]))
        dma("sync", "c_w", bqk[:, 0:2], t["bq"].rearrange("(m p) -> p m", p=P), slow=True)
        dma("sync", "c_w", bqk[:, 2:4], t["bk"].rearrange("(m p) -> p m", p=P), slow=True)
        m_w = dma("sync", "c_w", bvr[:, :], t["bv"].rearrange("(a n) -> a n", a=1).broadcast_to([P, D]))

        for g in range(1, 4):
            load_x(g)

        m_nhalf = pool(lambda e: e.memset(nhalf[:, :], -0.5))
        m_alibi = dma("gpsimd", "c_ali", Alid[:, :, :, :], t["c_alibi"])
        m_pad = [None] * 3

        def pad(i):
            m = ("gpsimd", pr.at["gpsimd"])
            if i == 0:
                m_pad[0] = pool(lambda e: e.memset(QO[64:96, :, :, :].bitcast(F32), 1.0), m)
            elif i == 1:
                pool(lambda e: e.memset(KO[64:96, :, :, :].bitcast(F32), 0.0), m)
            elif i == 2:
                m = pool(lambda e: e.memset(KO[96:98, :, :, :].bitcast(F32), 1.0), m)
                m_pad[1] = dma("sync", "c_one", KO[66:68, :, :, :].bitcast(F32), KO[96:98, :, :, :].bitcast(F32), m)
            elif i == 3:
                m_pad[2] = pool(lambda e: e.memset(VB[:, :], 0.0), m)
            elif i == 4:
                m_pad[2] = pool(lambda e: e.memset(
                    vb.rearrange("p b c (h d) -> p (b c) h d", d=32)[:, :, :, HD:HD + 1], 1.0), m_pad[2])

        xn_v = Xn.rearrange("(g j p) d -> g p j d", p=P, j=4)
        v_v = Vd.rearrange("(g j p) n -> g p j n", p=P, j=4)
        m_rstd, m_xnst, m_xev, m_xmm, m_qkst, m_vst, m_tr = {}, {}, {}, {}, {}, {}, {}
        free = {}
        px = [0]

        def take():
            bank = 5 + px[0] % 3
            px[0] += 1
            return bank


        m_wt = {}

        def split_weights():
            m_bq = dve(lambda e: e.tensor_scalar(bqk[:, 0:2], bqk[:, 0:2], SCALE, None, ALU.mult), m_w)
            a1 = act(lambda e: e.activation(Wqk["h"][:, 0, :, :], Wst[:, 0, :, :], ACT.Copy, scale=SCALE), m_w)
            a2 = act(lambda e: e.copy(Wqk["h"][:, 1, :, :], Wst[:, 1, :, :]))
            a3 = act(lambda e: e.copy(Wv["h"][:, :, :], Wvst[:, :, :]))
            a4 = act(lambda e: e.copy(WoH[:, :, :], Wost))
            m_wq = dve(lambda e: e.scalar_tensor_tensor(Wqk["l"][:, 0, :, :], Wst[:, 0, :, :], SCALE,
                                                        Wqk["h"][:, 0, :, :].bitcast(F32), ALU.mult, ALU.subtract), a1)
            m_wk = dve(lambda e: e.tensor_tensor(Wqk["l"][:, 1, :, :], Wst[:, 1, :, :],
                                                 Wqk["h"][:, 1, :, :].bitcast(F32), ALU.subtract), a2)
            m_wv = dve(lambda e: e.tensor_tensor(Wv["l"][:, :, :], Wvst[:, :, :], Wv["h"][:, :, :].bitcast(F32),
                                                 ALU.subtract), a3)
            m_wo = dve(lambda e: e.tensor_tensor(WoL[:, :, :], Wost, WoH[:, :, :].bitcast(F32),
                                                 ALU.subtract), a4)
            m_wt.update(bq=m_bq, qk=(m_wq, m_wk), v=m_wv, o=m_wo)

        NPAIR = NB * NH // 2
        m_ops, m_st_last, m_a_last, m_mrow = {}, {}, {}, {}

        def load_pair(r, part=None):
            b, j = divmod(r, NH // 2)
            k = r % 3
            nm = f"op{k}"
            at = slice(b * S, (b + 1) * S)
            if part in (None, 0):
                wait("sync", m_pad[0], m_pad[1], m_alibi, m_st_last.get(r - 3), m_a_last.get(r - 3), *m_qkst[2 * b], *m_qkst[2 * b + 1])
            for i in range(4) if part is None else (part,):
                dst, o, parts, al = ((QO, 0, (QKh, QKl, QKh, QKl), 1), (KO, D, (QKh, QKh, QKl, QKl), 0))[i // 2]
                for n in (0, 1) if i % 2 == 0 else (2, 3):
                    dma("sync", nm, dst[16 * n:16 * n + 16, k, :, :].bitcast(F32),
                        parts[n][o + 32 * j:o + 32 * j + 32, at].rearrange("(h d) n -> d h n", d=HD))
                if i % 2:
                    m_ops[r] = dma("sync", nm, dst[64 + 2 * al:66 + 2 * al, k, :, :].bitcast(F32),
                                   Alid[al, 2 * j:2 * j + 2, :, :].rearrange("h r n -> r h n"))

        m_mxfree = {}

        n_unit = [0]

        def score_max(bank=None):
            r, u = divmod(n_unit[0], 32)
            if r == NPAIR:
                return
            n_unit[0] += 1
            hh, i, half = u // 16, (u // 2) % 8, u % 2
            k = r % 3
            bank = take() if bank is None else bank
            q = mm(ps[:, bank, :], QO[0:96, k, hh, i * P:(i + 1) * P], KO[0:96, k, hh, half * GT:(half + 1) * GT],
                   True, True, m_ops[r], *free.get(bank, ()), sig=True)
            d = dve(lambda e: e.reduce_max(mx[:, r % 2, hh, i, half:half + 1], ps[:, bank, :], AX.X), q)
            free[bank] = (d,)
            if u == 31:
                m_a_last[r] = q
                k2 = r % 2
                m = dve(lambda e: e.tensor_reduce(m16[:, k2, :, :], mx[:, k2, :, :, :], AX.X, ALU.max), d)
                m1 = act(lambda e: e.activation(mneg[:, k2, :, 0, :].bitcast(F32R), m16[:, k2, :, :], ACT.Copy,
                                                scale=-1.0), m, m_mxfree.get(r - 2))
                m_mrow[r] = dve(lambda e: e.scalar_tensor_tensor(mneg[:, k2, :, 1, :], m16[:, k2, :, :], -1.0,
                                                                 mneg[:, k2, :, 0, :], ALU.mult, ALU.subtract), m1)

        m_max = {}

        def max_rows(r, bank=None):
            k2 = r % 2
            bank = take() if bank is None else bank
            q = transpose(ps[0:32, bank, 0:P], mneg[:, k2, :, :, :].rearrange("p h l i -> p (h l i)"),
                          m_mrow[r], m_ident, *free[bank], sig=True)
            m_mxfree[r] = q
            d = act(lambda e: e.copy(mT[:, k2, :], ps[0:32, bank, 0:P]), q, m_max.get(r - 2))
            free[bank] = (d,)
            for hh in range(2):
                m_max[r] = dma("sync", f"mx{k2}", QO[96:98, r % 3, hh, :].bitcast(F32).rearrange("l (i n) -> l i n", n=P),
                               mT[16 * hh:16 * hh + 16, k2, :].bitcast(F32), d)

        m_v, m_vst2, m_pv_batch = {}, {}, {}
        v_rows = Vd.rearrange("(b f c p) n -> b f p c n", p=P, c=4, f=2)

        def load_v(b, f):
            i = 2 * b + f
            ld = dma("gpsimd", "vst", vst[:, :, :], v_rows[b, f], m_vst2.get(i - 1), m_vst[2 * b + f])
            m_v[b] = m_vst2[i] = pool(lambda e: e.tensor_copy(
                vb[:, b % 2, 4 * f:4 * f + 4, :].rearrange("p c (h d) -> p c h d", d=32)[:, :, :, 0:HD],
                vst[:, :, :].rearrange("p c (h d) -> p c h d", d=HD)), ld, m_pad[2], m_pv_batch.get(b - 2))

        def layer_stats(g, half):
            k = g % 2
            for j in (2 * half, 2 * half + 1):
                s = dve(lambda e, j=j: e.bn_stats(stats[:, k, j, :], xt[:, g % 4, j, :]), m_x[g])
            if half:
                wait("vector", s)
                for j in range(4):
                    s = dve(lambda e, j=j: e.bn_aggr(mv[:, k, j, :], stats[:, k, j, :]))
                s = dve(lambda e: e.tensor_scalar(veps[:, k, :], mv[:, k, :, 1], EPS, None, ALU.add), s)
                m_rstd[g] = pool(lambda e: e.tensor_tensor(rstd[:, k, :], veps[:, k, :], nhalf[:, :], ALU.pow),
                                 s, m_nhalf, ("gpsimd", pr.at["gpsimd"]))

        def normalise(g, half):
            k = g % 2
            n = g % 3
            wait("vector", m_rstd[g], m_tr.get(g - 3), m_xnst.get(g - 3))
            for j in (2 * half, 2 * half + 1):
                s = dve(lambda e, j=j: e.tensor_scalar(xn[:, n, j, :], xt[:, g % 4, j, :], mv[:, k, j, 0:1],
                                                       rstd[:, k, j:j + 1], ALU.subtract, ALU.mult))
            if half:
                m_norm[g] = s
                m_xnst[g] = dma("sync", f"xn{n}", xn_v[g], xn[:, n, :, :], s)
                if g + 2 >= 4 and g + 2 < NG:
                    load_x(g + 2)

        def to_columns(src, banks, hi, lo, *m):
            wait("tensor", m_ident, *m, *free.get(banks[0], ()), *free.get(banks[1], ()))
            for c in range(2):
                for j in range(4):
                    tr = transpose(ps[:, banks[c], j * P:(j + 1) * P], src[:, j, c * P:(c + 1) * P],
                                   sig=c == 1 and j == 3)
            b = banks[0]
            a = act(lambda e: e.copy(hi, ps[:, b:b + 2, :]), tr)
            d = dve(lambda e: e.tensor_tensor(lo, ps[:, b:b + 2, :], hi.bitcast(F32), ALU.subtract), a)
            free[banks[0]] = free[banks[1]] = (a, d)
            return tr, (a, d)

        def columns(g):
            k = g % 2
            b = 2 * k
            wait("scalar", *m_xmm.get(g - 2, ()))
            wait("vector", *m_xmm.get(g - 2, ()))
            m_tr[g], m_xev[g] = to_columns(xn[:, g % 3, :, :], (b, b + 1), XH[:, k, :, :], XL[:, k, :, :], m_norm[g])

        ring_a = [0]

        def project(g, fills):
            k = g % 2
            wait("tensor", *m_xev[g], *m_wt["qk"], m_wt["v"])
            wait("scalar", *m_qkst.get(g - 2, ()), m_vst.get(g - 2), m_wt["bq"], m_wt["o"])
            wait("vector", *m_qkst.get(g - 2, ()), m_w)
            for o in range(4):
                bank = 4 + ring_a[0] % 3
                ring_a[0] += 1
                w, m0 = o // 2, (o % 2) * P
                q = mm3(ps[:, bank, :], [(Wqk["h"][:, w, c, m0:m0 + P], Wqk["l"][:, w, c, m0:m0 + P],
                                          XH[:, k, c, :], XL[:, k, c, :]) for c in range(2)],
                        *free.get(bank, ()), sig=True)
                a = act(lambda e, o=o, bank=bank: e.activation(qkH[:, k, o, :], ps[:, bank, :], ACT.Identity,
                                                               bias=bqk[:, o:o + 1]), q)
                d = dve(lambda e, o=o, bank=bank: e.scalar_tensor_tensor(
                    qkL[:, k, o, :], ps[:, bank, :], bqk[:, o:o + 1], qkH[:, k, o, :].bitcast(F32),
                    ALU.add, ALU.subtract), a)
                free[bank] = (a, d)
                fills[o]()
            at = slice(g * GT, (g + 1) * GT)
            s1 = dma("sync", f"qh{k}", QKh.rearrange("(o p) n -> p o n", p=P)[:, :, at], qkH[:, k, :, :].bitcast(F32), a)
            s2 = dma("sync", f"ql{k}", QKl.rearrange("(o p) n -> p o n", p=P)[:, :, at], qkL[:, k, :, :].bitcast(F32), d)
            m_qkst[g] = (s1, s2)
            for j in range(4):
                bank = 4 + ring_a[0] % 3
                ring_a[0] += 1
                q = mm3(ps[:, bank, 0:D + NE], [(XH[:, k, c, j * P:(j + 1) * P], XL[:, k, c, j * P:(j + 1) * P],
                                                 Wv["h"][:, c, :], Wv["l"][:, c, :]) for c in range(2)],
                        *free.get(bank, ()), sig=True)
                a = act(lambda e, j=j, bank=bank: e.copy(vs[:, k, j, :], ps[:, bank, 0:D + NE]), q)
                free[bank] = (a,)
                fills[4 + j]()
            m_xmm[g] = (q,)
            wait("gpsimd", ("gpsimd", pr.at["gpsimd"]))
            m = pool(lambda e: e.tensor_copy(Lg[:, 4 * g:4 * g + 4, :], vs[:, k, :, D:D + NE]), a)
            d = pool(lambda e: e.tensor_tensor(
                vs[:, k, :, 0:D], vs[:, k, :, 0:D],
                bvr[:, :].rearrange("p (u d) -> p u d", u=1).broadcast_to([P, 4, D]), ALU.add), m_w)
            m_vst[g] = dma("sync", f"vs{k}", v_v[g], vs[:, k, :, 0:D], d)
            return m

        AHEAD = 44
        FIRST = NG - AHEAD // 4
        layer_stats(0, 0)
        layer_stats(0, 1)
        layer_stats(1, 0)
        layer_stats(1, 1)
        for half in range(2):
            normalise(0, half)
        columns(0)
        split_weights()
        pad(0)
        layer_stats(2, 0)
        for half in range(2):
            normalise(1, half)
        layer_stats(2, 1)
        for g in range(NG):
            if g + 3 < NG:
                layer_stats(g + 3, 0)
            if g + 2 < NG:
                normalise(g + 2, 0)
            if g + 1 < NG:
                columns(g + 1)
            fills = [lambda: None] * 8
            if g + 2 < NG:
                fills[1] = lambda g=g: normalise(g + 2, 1)
            if g + 3 < NG:
                fills[3] = lambda g=g: layer_stats(g + 3, 1)
            if g >= FIRST:
                fills[0] = fills[2] = fills[5] = fills[7] = lambda: score_max(7)
            pad(g + 1)
            m_lg = project(g, fills)
            if g in (4, 5):
                load_v(0, g - 4)
            if g == FIRST + 8:
                max_rows(0, 7)
            if 2 <= g < 6:
                for i in (0, 1) if g % 2 == 0 else (2, 3):
                    load_pair(g // 2 - 1, i)
        done_a = [m_lg, *m_qkst[NG - 1], *m_qkst[NG - 2], m_vst[NG - 1], m_vst[NG - 2],
                  m_xnst[NG - 1], m_xnst[NG - 2], m_xnst[NG - 3], *m_xmm[NG - 1], m_wt["o"], m_w]
        A.close()

        B = ExitStack()
        NPT = 8
        pta = sbuf(B, "pta", [P, NPT // 2, S])
        WB = [sbuf(B, f"WB{i}", [P, 2 * RAW], F32R) for i in range(2)]
        ptb = sbuf(B, "ptb", [P, NPT // 2, S])
        accs = sbuf(B, "accs", [P, 2, GT])
        rc = sbuf(B, "rc", [P, 2, 4, 4])
        ot = sbuf(B, "ot", [P, 8, D])
        wraw = sbuf(B, "wraw", [P, RAW])
        zero = sbuf(B, "zero", [P, D])
        R = B
        rt = {n: sbuf(R, "r_" + n, [P, NT, NE]) for n in ("eq", "o1", "o2", "t", "pa", "pb")}
        rt["rk"] = rt["eq"]
        rs = {n: sbuf(R, "r_" + n, [P, NT]) for n in ("m1", "m2", "r", "s")}
        cnt = {n: sbuf(R, "r_" + n, [P, NE]) for n in ("nb", "ia", "ib", "base")}
        cmp16 = sbuf(R, "cmp16", [P, NE, 16])
        cmpb = sbuf(R, "cmpb", [P, NBLK, NE])
        bex = sbuf(R, "bex", [P, NBLK])
        tri = sbuf(R, "tri", [P, P])
        onesm = sbuf(R, "onesm", [P, P])
        crow = sbuf(R, "crow", [P, 8 + 16 + NBLK + 1])
        dma("gpsimd", "c_r", tri[:, :], t["c_tri"], *done_a)
        m_cr = dma("gpsimd", "c_r", crow[:, :], t["c_row"])
        m_ones = pool(lambda e: e.memset(onesm[:, :], 1.0), *done_a)
        m_zero = pool(lambda e: e.memset(zero[:, :], 0.0))
        m_wz = pool(lambda e: e.memset(wraw[:, W3_AT + 2 * D:RAW], 0.0))
        def over_tiles(a):
            return a.rearrange("p (u e) -> p u e", u=1).broadcast_to([P, NT, NE])

        def over_experts(a):
            return a.rearrange("p (n u) -> p n u", u=1).broadcast_to([P, NT, NE])

        rev = over_tiles(crow[:, 0:8])

        def tt(o, a, b, op, *m):
            return dve(lambda e: e.tensor_tensor(o, a, b, op), *m)

        def red(o, a, op, *m):
            return dve(lambda e: e.tensor_reduce(o, a, AX.X, op), *m)

        def first_of(best, one_hot, logits, m):
            m = red(best, logits, ALU.max, m)
            yield
            m = tt(rt["eq"][:, :, :], logits, over_experts(best), ALU.is_equal, m)
            yield
            m = tt(rt["t"][:, :, :], rt["eq"][:, :, :], rev, ALU.mult, m)
            yield
            m = red(rs["r"][:, :], rt["t"][:, :, :], ALU.max, m)
            yield
            return tt(one_hot, rt["t"][:, :, :], over_experts(rs["r"][:, :]), ALU.is_equal, m)

        routed = {}

        def route():
            wait("vector", *done_a, m_cr)
            m = yield from first_of(rs["m1"][:, :], rt["o1"][:, :, :], Lg[:, :, :], None)
            yield
            m = dve(lambda e: e.scalar_tensor_tensor(rt["pa"][:, :, :], rt["o1"][:, :, :], -3.0e38, Lg[:, :, :],
                                                     ALU.mult, ALU.add), m)
            yield
            m = yield from first_of(rs["m2"][:, :], rt["o2"][:, :, :], rt["pa"][:, :, :], m)
            yield
            m_d = tt(rs["s"][:, :], rs["m2"][:, :], rs["m1"][:, :], ALU.subtract, m)
            yield
            m_e = act(lambda e: e.activation(rs["s"][:, :], rs["s"][:, :], ACT.Exp), m_d)
            yield
            m_m = tt(rt["eq"][:, :, :], rt["o1"][:, :, :], rt["o2"][:, :, :], ALU.add, m)
            yield
            m = dve(lambda e: e.tensor_scalar(rs["r"][:, :], rs["s"][:, :], 1.0, None, ALU.add), m_e, m_m)
            yield
            m = dve(lambda e: e.reciprocal(prob[:, 0, :], rs["r"][:, :]), m)
            yield
            routed["prob"] = tt(prob[:, 1, :], rs["s"][:, :], prob[:, 0, :], ALU.mult, m)
            flat = rt["eq"][:, :, :].rearrange("p n e -> p (n e)")
            bk0, bk1 = take(), take()
            mm(ps[:, bk0, :], tri[:, :], flat, True, True, m_m, m_cr, m_ones, *free[bk0])
            mr = mm(ps[:, bk1, :], onesm[:, :], flat, True, True, *free[bk1], sig=True)
            b0 = ps[:, bk0, :].rearrange("p (n e) -> p n e", e=NE)
            b1 = ps[:, bk1, :].rearrange("p (n e) -> p n e", e=NE)
            m = dve(lambda e: e.tensor_copy(rt["rk"][:, :, :], b0), mr)
            free[bk0] = (m,)
            dve(lambda e: e.tensor_copy(rt["pa"][:, :, :], b1))
            m = tt(rt["rk"][:, :, :], rt["rk"][:, :, :], b1, ALU.subtract, m)
            free[bk1] = (m,)
            a, b = rt["pa"], rt["pb"]
            sh = 1
            while sh < NT:
                m = dve(lambda e, a=a, b=b, sh=sh: e.tensor_copy(b[:, 0:sh, :], a[:, 0:sh, :]), m)
                yield
                m = tt(b[:, sh:NT, :], a[:, sh:NT, :], a[:, 0:NT - sh, :], ALU.add, m)
                yield
                a, b = b, a
                sh *= 2
            total = a[:, NT - 1, :]
            m2 = tt(cmp16[:, :, :], total.rearrange("p (e u) -> p e u", u=1).broadcast_to([P, NE, 16]),
                    crow[:, 8:24].rearrange("p (u j) -> p u j", u=1).broadcast_to([P, NE, 16]), ALU.is_gt, m)
            yield
            m2 = red(cnt["nb"][:, :], cmp16[:, :, :], ALU.add, m2)
            yield
            ia, ib = cnt["ia"], cnt["ib"]
            m2 = dve(lambda e: e.tensor_copy(cnt["ia"][:, :], cnt["nb"][:, :]), m2)
            yield
            sh = 1
            while sh < NE:
                m2 = dve(lambda e, ia=ia, ib=ib, sh=sh: e.tensor_copy(ib[:, 0:sh], ia[:, 0:sh]), m2)
                yield
                m2 = tt(ib[:, sh:NE], ia[:, sh:NE], ia[:, 0:NE - sh], ALU.add, m2)
                yield
                ia, ib = ib, ia
                sh *= 2
            m3 = tt(cnt["base"][:, :], ia[:, :], cnt["nb"][:, :], ALU.subtract, m2)
            yield
            m4 = tt(cmpb[:, :, :], crow[:, 24:24 + NBLK].rearrange("p (b u) -> p b u", u=1).broadcast_to([P, NBLK, NE]),
                    ia[:, :].rearrange("p (u e) -> p u e", u=1).broadcast_to([P, NBLK, NE]), ALU.is_ge, m3)
            yield
            m4 = red(bex[:, :], cmpb[:, :, :], ALU.add, m4)
            yield
            m4 = dve(lambda e: e.tensor_scalar(bex[:, :], bex[:, :], float(NE - 1), float(P), ALU.min, ALU.mult), m4)
            yield
            routed["widx"] = dve(lambda e: e.tensor_scalar(widx[:, :], bex[:, :], crow[:, 24 + NBLK:25 + NBLK], None, ALU.add), m4)
            m = tt(b[:, :, :], a[:, :, :], rt["rk"][:, :, :], ALU.add, m4)
            yield
            m = dve(lambda e, b=b: e.scalar_tensor_tensor(b[:, :, :], over_tiles(cnt["base"][:, :]), float(GT), b[:, :, :],
                                                          ALU.mult, ALU.add), m)
            yield
            m = tt(rt["t"][:, :, :], b[:, :, :], rt["o1"][:, :, :], ALU.mult, m)
            yield
            m = red(rs["m1"][:, :], rt["t"][:, :, :], ALU.add, m)
            yield
            m = dve(lambda e: e.tensor_copy(slot[:, 0, :], rs["m1"][:, :]), m)
            yield
            m = tt(rt["t"][:, :, :], b[:, :, :], rt["o2"][:, :, :], ALU.mult, m)
            yield
            m = red(rs["m2"][:, :], rt["t"][:, :, :], ALU.add, m)
            yield
            routed["slot"] = dve(lambda e: e.tensor_copy(slot[:, 1, :], rs["m2"][:, :]), m)

        def scatter_group(g, last=[None, None]):
            k = g % 2
            ld = dma("gpsimd", f"xg{k}", xr[:, k, :, :], xn_v[g], last[k], *done_a)
            wait("gpsimd", ld, routed["slot"], m_zs[0])
            nm = f"sc{k}"
            s = pr.sem(nm)
            for i in range(4):
                for c in range(2):
                    pr.at[nm] += 16
                    pr.queues["gpsimd"].append(lambda e, i=i, c=c: e.indirect_dma_start(
                        Xs[:, :], bass.IndirectOffsetOnAxis(ap=slot[:, c, 4 * g + i:4 * g + i + 1], axis=0),
                        xr[:, k, i, :], None).then_inc(s, 16))
            last[k] = (nm, pr.at[nm])
            m_scat[k] = last[k]

        m_scat, m_zs = [None, None], [None]

        def clear_slots(b):
            m_zs[0] = dma("gpsimd", "zero", Xs[b * GT:(b + 1) * GT, :].rearrange("(p j) d -> p j d", p=P),
                          zero[:, :].rearrange("p (u d) -> p u d", u=1).broadcast_to([P, 4, D]), m_zero)

        def wsource(e):
            if e < NE:
                return t["W1"][e], t["W2"][e], t["W3"][e]
            a = (e - NE) * HE
            return t["Ws1"][:, a:a + HE], t["Ws2"][:, a:a + HE], t["Ws3"][a:a + HE, :]

        m_wraw, m_split, m_wstore = {}, {}, {}

        def load_expert(e):
            w1, w2, w3 = wsource(e)
            wait("gpsimd", *m_split.get(e - 1, ()), m_wz)
            dma("gpsimd", "wraw", wraw[:, 0:W2_AT].rearrange("p (c n) -> p c n", c=2), rows(w1))
            dma("gpsimd", "wraw", wraw[:, W2_AT:W3_AT].rearrange("p (c n) -> p c n", c=2), rows(w2))
            dma("gpsimd", "wraw", wraw[:, W3_AT:W3_AT + 2 * D].rearrange("p (c n) -> p c n", c=2), rows(w3[0:2 * P, :]))
            m_wraw[e] = dma("gpsimd", "wraw", wraw[0:96, W3_AT + 2 * D:RAW], w3[2 * P:HE, :])

        def split_expert(e):
            w = WB[e % 2]
            a = act(lambda q: q.copy(w[:, 0:RAW], wraw[:, :]), m_wraw[e], m_wz, m_wstore.get(e - 2), *done_a)
            b = pool(lambda q: q.tensor_tensor(w[:, RAW:2 * RAW], wraw[:, :], w[:, 0:RAW].bitcast(F32),
                                               ALU.subtract), a)
            m_split[e] = (a, b)

        def store_expert(e):
            m_wstore[e] = dma("gpsimd", f"wst{e % 2}", Wd[e * P:(e + 1) * P, :], WB[e % 2][:, :].bitcast(F32),
                              *m_split[e])

        def pt(s):
            return pta[:, s, :] if s < NPT // 2 else ptb[:, s - NPT // 2, :]

        m_exp, m_pv, m_pfree, m_acc = {}, {}, {}, {}
        n_exp = [0]
        p_of = {}

        def scores(r, kc, hh, half):
            k = r % 3
            n = n_exp[0]
            b0_ = 2 * (n % 2)
            q = mm(ps[:, b0_ + half, :], KO[0:98, k, hh, kc * P:(kc + 1) * P], QO[0:98, k, hh, half * GT:(half + 1) * GT],
                   True, True, m_ops[r], m_max[r], *free[b0_ + half], sig=half == 1)
            if half == 0:
                return
            n_exp[0] += 1
            if kc == 7 and hh == 1:
                m_st_last[r] = q
            s = n % NPT
            p_of[r, kc, hh] = s
            a = act(lambda e: e.activation(pt(s), ps[:, b0_:b0_ + 2, :], ACT.Exp), q, m_pfree.get(s),
                    *(done_a if s >= NPT // 2 else ()))
            free[b0_] = free[b0_ + 1] = (a,)
            m_exp[r, kc, hh] = a

        def values(r, kc):
            b, j = divmod(r, NH // 2)
            wait("tensor", m_exp[r, kc, 0], m_exp[r, kc, 1], m_v[b], *(free[4] if kc == 0 else ()))
            for hh in range(2):
                for half in range(2):
                    g4 = 2 * hh + half
                    q = mm(ps[32 * g4:32 * g4 + 32, 4, :], vb[:, b % 2, kc, 32 * (2 * j + hh):32 * (2 * j + hh) + 32],
                           pt(p_of[r, kc, hh])[:, half * GT:(half + 1) * GT], kc == 0, kc == 7, sig=g4 == 3)
            for hh in range(2):
                m_pfree[p_of[r, kc, hh]] = q
            if kc == 7:
                m_pv_batch[b] = q
                k2 = r % 2
                a = act(lambda e: e.copy(accs[:, k2, :], ps[:, 4, :]), q, m_acc.get(r - 2), *done_a)
                free[4] = (a,)
                m_pv[r] = a

        m_ot, m_od = {}, {}

        def normalise_heads(r):
            b, j = divmod(r, NH // 2)
            k2 = r % 2
            bank = take()
            wait("tensor", m_pv[r], *free[bank])
            for c in range(4):
                q = transpose(ps[:, bank, c * P:(c + 1) * P], accs[:, k2, c * P:(c + 1) * P], sig=c == 3)
            a = act(lambda e: e.copy(accs[:, k2, :], ps[:, bank, :]), q)
            free[bank] = (a,)
            v = accs[:, k2, :].rearrange("p (c g d) -> p c g d", c=4, g=4)
            m = dve(lambda e: e.reciprocal(rc[:, k2, :, :], v[:, :, :, HD]), a)
            wait("gpsimd", m, m_od.get(b - 1))
            for hh in range(2):
                h = 2 * j + hh
                o = ot[:, :, HD * h:HD * h + HD].rearrange("p (f c) d -> p c f d", f=2)
                m = pool(lambda e, hh=hh, o=o: e.tensor_tensor(
                    o, v[:, :, 2 * hh:2 * hh + 2, 0:HD],
                    rc[:, k2, :, 2 * hh:2 * hh + 2].rearrange("p c (g u) -> p c g u", u=1).broadcast_to([P, 4, 2, HD]),
                    ALU.mult))
            m_acc[r] = m
            if j == NH // 2 - 1:
                m_od[b] = dma("sync", "od", Od.rearrange("(b c p) d -> b p c d", p=P, c=8)[b],
                              ot[:, :, :], m)

        load_pair(2)
        routing = route()
        LAG = 2

        def b_step(s):
            r, kc = divmod(s, 8)
            for hh in range(2):
                if r < NPAIR:
                    scores(r, kc, hh, 0)
                    scores(r, kc, hh, 1)
                score_max()
            score_max()
            if s >= LAG:
                values(*divmod(s - LAG, 8))
            score_max()
            if s >= LAG + 8 and (s - LAG) % 8 == 0:
                normalise_heads((s - LAG) // 8 - 1)
            if kc == 5 and r + 1 < NPAIR:
                max_rows(r + 1)
            if kc == 0 and r >= 1 and r + 2 < NPAIR:
                load_pair(r + 2)
            if r < NE + 2:
                if kc == 1:
                    load_expert(r)
                if kc == 4:
                    split_expert(r)
                if kc == 7:
                    store_expert(r)
            if 4 * r + kc < NBLK and kc < 4:
                clear_slots(4 * r + kc)
            if kc == 3 and 34 <= r < 34 + NG:
                scatter_group(r - 34)
            if kc == 5 and r % 8 in (2, 3) and r < NPAIR - 8:
                load_v(r // 8 + 1, r % 8 - 2)
            if s % 4 == 3:
                next(routing, None)

        for s in range(8 * NPAIR - 8):
            b_step(s)
        for _ in routing:
            pass
        m_slot, m_widx, m_prob = routed["slot"], routed["widx"], routed["prob"]
        B.close()

        C = ExitStack()
        OH, OL = (sbuf(C, n, [P, 2, GT], F32R) for n in ("OH", "OL"))
        gath = sbuf(C, "gath", [P, 4, 2, D])
        WB_ = [sbuf(C, f"WB{i}c", [P, 2 * RAW], F32R) for i in range(2)]
        WB = WB + [sbuf(C, "WB2", [P, 2 * RAW], F32R)]
        CH = OPS[:, 8192:10240].rearrange("p (b c n) -> p b c n", b=2, c=2)
        CL = OPS[:, 10240:12288].rearrange("p (b c n) -> p b c n", b=2, c=2)
        HH = OPS[:, 0:4096].rearrange("p (s n) -> p s n", s=8)
        HL = OPS[:, 4096:8192].rearrange("p (s n) -> p s n", s=8)
        orow = VB[:, 0:1024].rearrange("p (j d) -> p j d", j=4)
        sg = VB[:, 1024:2048].rearrange("p (b n) -> p b n", b=2)
        hf = VB[:, 2048:3072].rearrange("p (b n) -> p b n", b=2)
        yr = VB[:, 3072:5120].rearrange("p (b j d) -> p b j d", b=2, j=4)
        xres = VB[:, 5120:6144].rearrange("p (j d) -> p j d", j=4)
        gu = [0]
        nh = [0]
        m_wb, m_wbfree, m_xr, m_xcol, m_xused, m_xrfree = {}, {}, {}, {}, {}, {}
        m_h, m_hfree, m_sg, m_hf = {}, {}, {}, {}

        def gate_up(xh, xl, w, hc, *m):
            h0, hn = HC[hc]
            n = nh[0]
            nh[0] += 1
            s, k = n % 8, n % 2
            banks = (2 + 2 * (n % 2), 3 + 2 * (n % 2))
            wait("tensor", *m)
            for which, bank in zip((0, W2_AT), banks):
                ks = []
                for c in range(2):
                    a = which + c * HE + h0
                    ks.append((w[:, a:a + hn], w[:, RAW + a:RAW + a + hn], xh[:, c, :], xl[:, c, :]))
                q = mm3(ps[0:hn, bank, :], ks, *free[bank], sig=True)
                if which == 0:
                    a_ = act(lambda e: e.activation(sg[0:hn, k, :], ps[0:hn, banks[0], :], ACT.Silu), q, m_hf.get(n - 2))
                    free[banks[0]] = (a_,)
            d = dve(lambda e: e.tensor_tensor(hf[0:hn, k, :], ps[0:hn, banks[1], :], sg[0:hn, k, :], ALU.mult),
                    q, a_, *m_h.get(n - 2, ()))
            free[banks[1]] = (d,)
            m_hf[n] = d
            a2 = act(lambda e: e.copy(HH[0:hn, s, :], hf[0:hn, k, :]), d, m_hfree.get(s))
            d2 = dve(lambda e: e.tensor_tensor(HL[0:hn, s, :], hf[0:hn, k, :], HH[0:hn, s, :].bitcast(F32),
                                               ALU.subtract), a2)
            m_h[n] = (a2, d2)
            return n

        def down(chunks, extra=()):
            for j in range(4):
                col = slice(j * P, (j + 1) * P)
                ks = []
                for w, hc, n in chunks:
                    hn = HC[hc][1]
                    a = W3_AT + hc * D
                    wait("tensor", *m_h[n])
                    ks.append((HH[0:hn, n % 8, col], HL[0:hn, n % 8, col], w[0:hn, a:a + D], w[0:hn, RAW + a:RAW + a + D]))
                for xh, xl, wh, wl in extra:
                    ks.append((xh[:, col], xl[:, col], wh, wl))
                q = mm3(ps[:, 6 + j // 2, (j % 2) * D:(j % 2) * D + D], ks, *free[6 + j // 2], sig=j == 3)
            for _, _, n in chunks:
                m_hfree[n % 8] = q
            return q

        m_yr = {}
        xs_v = Xs.rearrange("(b j p) d -> b p j d", p=P, j=4)
        ys_v = Ys.rearrange("(b j p) d -> b p j d", p=P, j=4)

        def gather_weights(b):
            k = b % 3
            wait("gpsimd", m_widx, m_wbfree.get(b - 3), m_wstore[NE + 1], m_wstore[NE], *(done_b if k == 2 else ()))
            nm = f"wb{k}"
            s = pr.sem(nm)
            pr.at[nm] += 16
            pr.queues["gpsimd"].append(lambda e: e.indirect_dma_start(
                WB[k][:, :].bitcast(F32), None, Wd[:, :],
                bass.IndirectOffsetOnAxis(ap=widx[:, b:b + 1], axis=0)).then_inc(s, 16))
            m_wb[b] = (nm, pr.at[nm])

        def load_slots(b):
            m_xr[b] = dma("sync", f"xr{b % 2}", xr[:, b % 2, :, :], xs_v[b], m_xrfree.get(b - 2), *m_scat, m_zs[0])

        def slot_columns(b):
            k = b % 2
            wait("scalar", m_xused.get(b - 2))
            wait("vector", m_xused.get(b - 2))
            m_xrfree[b], m_xcol[b] = to_columns(xr[:, k, :, :], (0, 1), CH[:, k, :, :], CL[:, k, :, :], m_xr[b])

        h_of = {}

        def block_up(b, hc):
            k = b % 2
            h_of[b, hc] = gate_up(CH[:, k, :, :], CL[:, k, :, :], WB[b % 3], hc, *m_xcol[b], m_wb[b])
            m_xused[b] = ("tensor", pr.at["tensor"])

        def block_down(b):
            q = down([(WB[b % 3], hc, h_of[b, hc]) for hc in range(3)])
            m_wbfree[b] = q
            k = b % 2
            a = act(lambda e: e.copy(yr[:, k, :, :].rearrange("p j d -> p (j d)"),
                                     ps[:, 6:8, :].rearrange("p a n -> p (a n)")), q, m_yr.get(b - 2))
            free[6] = free[7] = (a,)
            m_yr[b] = dma("sync", f"yr{k}", ys_v[b], yr[:, k, :, :], a)

        ms = {}

        def load_shared(i):
            ms[i] = dma("sync", f"ws{i}", WB[i][:, :].bitcast(F32), Wd[(NE + i) * P:(NE + i + 1) * P, :],
                        m_wbfree[NBLK - 3 + i], m_wstore[NE + 1], m_wstore[NE])

        od_v = Od.rearrange("(g j p) d -> g p j d", p=P, j=4)
        out_v = out.rearrange("b s d -> (b s) d").rearrange("(g j p) d -> g p j d", p=P, j=4)
        m_xr2, m_or, m_orfree, m_oc, m_gf, m_g, m_res, m_resf = {}, {}, {}, {}, {}, {}, {}, {}
        base = NBLK

        def load_rows(g):
            k = (base + g) % 2
            m_xr[base + g] = dma("sync", f"xr{k}", xr[:, k, :, :], xn_v[g], m_xrfree.get(base + g - 2))

        def load_o(g):
            m_or[g] = dma("sync", "or", orow, od_v[g], m_orfree.get(g - 1) if g else m_pv[NPAIR - 1], m_od[NB - 1])

        def o_columns(g):
            wait("scalar", m_xused.get(base + g - 1))
            wait("vector", m_xused.get(base + g - 1), )
            if g == 0:
                wait("scalar", *done_b)
                wait("vector", *done_b)
            wait("scalar", m_ydone.get(g - 1))
            wait("vector", m_ydone.get(g - 1))
            m_orfree[g], m_oc[g] = to_columns(orow, (0, 1), OH[:, :, :], OL[:, :, :], m_or[g])

        m_ydone = {}
        m_out = {}

        def gather_rows(g, j):
            i = 4 * g + j
            wait("gpsimd", m_yr[NBLK - 1], m_yr[NBLK - 2], m_gf.get(i - 4), m_prob)
            nm = f"ga{j}"
            for c in range(2):
                s = pr.sem(nm)
                pr.at[nm] += 16
                pr.queues["gpsimd"].append(lambda e, c=c, s=s: e.indirect_dma_start(
                    gath[:, j, c, :], None, Ys[:, :],
                    bass.IndirectOffsetOnAxis(ap=slot[:, c, i:i + 1], axis=0)).then_inc(s, 16))
            m_g[i] = (nm, pr.at[nm])

        def load_res(g):
            m_res[g] = dma("sync", "res", xres, x_v[g], m_resf.get(g - 1) if g else m_pv[NPAIR - 1])

        def shared_up(g, e, hc):
            k = (base + g) % 2
            h_of[base + g, e, hc] = gate_up(CH[:, k, :, :], CL[:, k, :, :], WB[e], hc, *m_xcol[base + g], ms[e])
            m_xused[base + g] = ("tensor", pr.at["tensor"])

        def shared_down(g):
            q = down([(WB[e], hc, h_of[base + g, e, hc]) for e in range(2) for hc in range(3)],
                     [(OH[:, c, :], OL[:, c, :], WoH[:, c, :], WoL[:, c, :]) for c in range(2)])
            m_ydone[g] = q
            k = g % 2
            wait("vector", q, m_yr.get(base + g - 2), m_prob)
            for j in range(4):
                i = 4 * g + j
                s1 = dve(lambda e, j=j, i=i: e.scalar_tensor_tensor(
                    yr[:, k, j, :], gath[:, j, 0, :], prob[:, 0, i:i + 1], ps[:, 6 + j // 2, (j % 2) * D:(j % 2) * D + D],
                    ALU.mult, ALU.add), m_g[i])
            free[6] = free[7] = (s1,)
            wait("vector", s1)
            for j in range(4):
                i = 4 * g + j
                m_gf[i] = dve(lambda e, j=j, i=i: e.scalar_tensor_tensor(
                    yr[:, k, j, :], gath[:, j, 1, :], prob[:, 1, i:i + 1], yr[:, k, j, :], ALU.mult, ALU.add))
            b = pool(lambda e: e.tensor_tensor(xres, xres, bor[:, :].rearrange("p (u d) -> p u d", u=1).broadcast_to(
                [P, 4, D]), ALU.add), m_res[g], m_bor)
            a = pool(lambda e: e.tensor_tensor(yr[:, k, :, :], yr[:, k, :, :], xres, ALU.add), m_gf[4 * g + 3], b)
            m_resf[g] = a
            m_yr[base + g] = m_out[g] = dma("sync", f"yr{k}", out_v[g], yr[:, k, :, :], a)

        gather_weights(0)
        gather_weights(1)
        load_slots(0)
        load_slots(1)
        for s in range(8 * NPAIR - 8, 8 * NPAIR):
            b_step(s)
        slot_columns(0)
        for s in range(8 * NPAIR, 8 * NPAIR + LAG):
            b_step(s)
        block_up(0, 0)
        normalise_heads(NPAIR - 1)
        done_b = [m_od[NB - 1], m_pv[NPAIR - 1], m_acc[NPAIR - 1], m_v[NB - 1]]
        for b in range(NBLK + 1):
            if 0 < b < NBLK:
                block_up(b, 0)
            if b == NBLK:
                shared_up(0, 0, 0)
            if b >= 1:
                block_down(b - 1)
            if b < NBLK:
                block_up(b, 1)
                slot_columns(b + 1)
                block_up(b, 2)
            if b + 2 < NBLK:
                gather_weights(b + 2)
                load_slots(b + 2)
            if b == NBLK - 2:
                load_shared(0)
                load_rows(0)
            if b == NBLK - 1:
                load_shared(1)
                load_rows(1)
                load_o(0)
                load_res(0)

        for j in range(4):
            gather_rows(0, j)
        for g in range(NG + 1):
            if 0 < g < NG:
                shared_up(g, 0, 0)
            if g >= 1:
                shared_down(g - 1)
            if g < NG:
                shared_up(g, 0, 1)
                o_columns(g)
                shared_up(g, 0, 2)
            if 1 <= g < NG:
                load_res(g)
                for j in range(4):
                    gather_rows(g, j)
            if g < NG:
                if g + 1 < NG:
                    load_o(g + 1)
                shared_up(g, 1, 0)
                if g + 1 < NG:
                    slot_columns(base + g + 1)
                shared_up(g, 1, 1)
                shared_up(g, 1, 2)
                if g + 2 < NG:
                    load_rows(g + 2)
        wait("sync", m_out[NG - 1], m_out[NG - 2])
        C.close()
        block = ctx.enter_context(nc.Block())
        pr.emit(block)


def constants():
    slopes = (1.0 / 2.0 ** (np.arange(NH, dtype=np.float32) / NH)).astype(np.float32)
    k = np.arange(S, dtype=np.float32) - (S - 1)
    alibi = np.stack([slopes[:, None] * k[None, :], slopes[:, None] * -k[None, :]]).astype(np.float32)
    first = (alibi.view(np.uint32) & np.uint32(0xFFFFF000)).view(np.float32)
    alibi = np.stack([first, alibi - first], axis=2)
    tri = np.triu(np.ones((P, P), np.float32), 1)
    row = np.concatenate([8.0 - np.arange(8), 512.0 * np.arange(16), np.arange(NBLK), [0.0]]).astype(np.float32)
    row = np.tile(row[None, :], (P, 1))
    row[:, -1] = np.arange(P)
    return {"c_ident": np.eye(P, dtype=np.float32), "c_alibi": alibi, "c_tri": tri, "c_row": row}


_NAMES = {"L0_attn_x": "x", "L0_attn_Wq": "Wq", "L0_attn_bq": "bq", "L0_attn_Wk": "Wk", "L0_attn_bk": "bk",
          "L0_attn_Wv": "Wv", "L0_attn_bv": "bv", "L0_attn_Wo": "Wo", "L0_attn_bo": "bo", "L0_ffn_Wg": "Wg",
          "L0_ffn_W1": "W1", "L0_ffn_W2": "W2", "L0_ffn_W3": "W3", "L0_ffn_Ws1": "Ws1", "L0_ffn_Ws2": "Ws2",
          "L0_ffn_Ws3": "Ws3"}


def kernel(**inputs):
    import concourse.bacc as _bacc
    from concourse.bass_utils import run_bass_kernel_spmd as _run

    nc = _bacc.Bacc("TRN2", target_bir_lowering=False, num_devices=1)
    arrays, t = {}, {}
    named = {short: np.ascontiguousarray(inputs[name]) for name, short in _NAMES.items()}
    named.update(constants())
    for short, a in named.items():
        arrays[f"in_{short}"] = a
        t[short] = nc.dram_tensor(f"in_{short}", a.shape, mybir.dt.from_np(a.dtype), kind="ExternalInput").ap()
    out = nc.dram_tensor("out_0", (NB, S, D), F32, kind="ExternalOutput").ap()
    build(nc, t, out)
    r = _run(nc, [arrays], core_ids=[0])
    return r.results[0]["out_0"]
```

```python
from contextlib import ExitStack

import numpy as np

import concourse.bass as bass
from concourse import mybir

F32 = mybir.dt.float32
F32R = mybir.dt.float32r
I32 = mybir.dt.int32
U32 = mybir.dt.uint32
ALU = mybir.AluOpType
ACT = mybir.ActivationFunctionType
AX = mybir.AxisListType

P = 128
NB, S, D = 8, 1024, 256
N = NB * S
NH, HD = 16, 16
NE, HE = 8, 352
HC = ((0, 128), (128, 128), (256, 96))
GT = 512
NG = N // GT
NT = N // P
BT = 256
NBLK = (2 * N - NE) // BT + NE
NSLOT = NBLK * BT
NCMP = N // BT
RAW = 4 * HE + 3 * D
W2_AT, W3_AT = 2 * HE, 4 * HE
SCALE = float(HD) ** -0.5
EPS = 1e-5


class Program:

    def __init__(self, nc, ctx):
        self.nc, self.ctx = nc, ctx
        self.queues = {e: [] for e in ("tensor", "vector", "scalar", "gpsimd", "sync")}
        self.sems, self.at, self.waited = {}, {}, {}

    def sem(self, name):
        if name not in self.sems:
            self.sems[name] = self.ctx.enter_context(self.nc.semaphore("s_" + name))
            self.at[name] = 0
        return self.sems[name]

    def wait(self, eng, *marks):
        for m in marks:
            if m is None:
                continue
            name, value = m
            if self.waited.get((eng, name), 0) < value:
                self.waited[eng, name] = value
                self.queues[eng].append(lambda e, s=self.sems[name], v=value: e.wait_ge(s, v))

    def put(self, eng, fn, *marks, sig=True):
        self.wait(eng, *marks)
        if not sig:
            self.queues[eng].append(fn)
            return None
        s = self.sem(eng)
        self.at[eng] += 1
        self.queues[eng].append(lambda e: fn(e).then_inc(s, 1))
        return eng, self.at[eng]

    def dma(self, eng, slot, out, in_, *marks, slow=False):
        self.wait(eng, *marks)
        s = self.sem(slot)
        self.at[slot] += 16
        self.queues[eng].append(
            lambda e: e.dma_start(out, in_, allow_slow_non_contiguous=slow).then_inc(s, 16))
        return slot, self.at[slot]

    def emit(self, block):
        for name, queue in self.queues.items():
            def run(e, queue=queue):
                for fn in queue:
                    fn(e)
            blocks = {"tensor": block.tensor, "vector": block.vector, "scalar": block.scalar,
                            "gpsimd": block.gpsimd, "sync": block.sync}
            blocks[name](run)


def build(nc, t, out):
    ctx = ExitStack()
    with ctx:
        pr = Program(nc, ctx)
        put, dma, wait = pr.put, pr.dma, pr.wait
        pe = lambda fn, *m, sig=False: put("tensor", fn, *m, sig=sig)
        dve = lambda fn, *m: put("vector", fn, *m)
        act = lambda fn, *m: put("scalar", fn, *m)
        pool = lambda fn, *m: put("gpsimd", fn, *m)

        def sbuf(stack, name, shape, dt=F32):
            return stack.enter_context(nc.sbuf_tensor(name, shape, dt))

        def dram(name, shape):
            return nc.dram_tensor(name, shape, F32).ap()

        ps = ctx.enter_context(nc.psum_tensor("ps", [P, 8, 512], F32))

        Xn = dram("Xn", [N, D])
        QKh = dram("QKh", [2 * D, N])
        QKl = dram("QKl", [2 * D, N])
        Vd = dram("Vd", [N, D])
        Alid = dram("Alid", [2, NH, 2, S])
        Wd = dram("Wd", [(NE + 2) * P, RAW])
        Xs = dram("Xs", [NSLOT, D])
        Ys = dram("Ys", [NSLOT, D])
        Od = dram("Od", [N, D])

        def mm(o, l, r, start, stop, *m, sig=False):
            return pe(lambda e: e.matmul(o, l, r, start=start, stop=stop), *m, sig=sig)

        def mm3(o, ks, *m, sig=False, first=True, last=True):
            wait("tensor", *m)
            n = 3 * len(ks)
            i = 0
            for lh, ll, rh, rl in ks:
                for l, r in ((ll, rh), (lh, rl), (lh, rh)):
                    end = i == n - 1
                    mark = mm(o, l, r, first and i == 0, last and end, sig=sig and end)
                    i += 1
            return mark

        def transpose(o, in_, *m, sig=False):
            return pe(lambda e: e.transpose(o, in_, ident[:, :]), *m, sig=sig)

        ident = sbuf(ctx, "ident", [P, P])
        WoH, WoL = (sbuf(ctx, n, [P, 2, D], F32R) for n in ("WoH", "WoL"))
        bor = sbuf(ctx, "bor", [P, D])
        Lg = sbuf(ctx, "Lg", [P, NT, NE])
        prob = sbuf(ctx, "prob", [P, 2, NT])
        slot = sbuf(ctx, "slot", [P, 2, NT], I32)
        widx = sbuf(ctx, "widx", [P, NBLK], I32)
        vst = sbuf(ctx, "vst", [P, 4, D])
        mx = sbuf(ctx, "mx", [P, 2, 2, 8, 2])
        m16 = sbuf(ctx, "m16", [P, 2, 2, 8])
        mneg = sbuf(ctx, "mneg", [P, 2, 2, 2, 8])
        mT = sbuf(ctx, "mT", [32, 2, P], F32R)
        xr = sbuf(ctx, "xr", [P, 2, 4, D])
        OPS = sbuf(ctx, "OPS", [P, 12 * S], F32R)
        QO = OPS[:, 0:6 * S].rearrange("p (k h n) -> p k h n", k=3, h=2)
        KO = OPS[:, 6 * S:12 * S].rearrange("p (k h n) -> p k h n", k=3, h=2)
        VB = sbuf(ctx, "VB", [P, 8 * S])
        vb = VB[:, :].rearrange("p (b c n) -> p b c n", b=2, c=8)

        m_ident = dma("sync", "c_ident", ident[:, :], t["c_ident"])
        m_bor = dma("sync", "c_bor", bor[:, :], t["bo"].rearrange("(a n) -> a n", a=1).broadcast_to([P, D]))

        A = ExitStack()
        Wst = sbuf(A, "Wst", [P, 2, 2, D])
        Wqk = {k: sbuf(A, "W" + k, [P, 2, 2, D], F32R) for k in ("h", "l")}
        Wvst = sbuf(A, "Wvst", [P, 2, D + NE])
        Wv = {k: sbuf(A, "Wv" + k, [P, 2, D + NE], F32R) for k in ("h", "l")}
        bqk = sbuf(A, "bqk", [P, 4])
        bvr = sbuf(A, "bvr", [P, D])
        nhalf = sbuf(A, "nhalf", [P, 4])
        xt = sbuf(A, "xt", [P, 4, 4, D])
        stats = sbuf(A, "stats", [P, 2, 4, 6])
        mv = sbuf(A, "mv", [P, 2, 4, 2])
        veps = sbuf(A, "veps", [P, 2, 4])
        rstd = sbuf(A, "rstd", [P, 2, 4])
        xn = sbuf(A, "xn", [P, 3, 4, D])
        XH, XL = (sbuf(A, n, [P, 2, 2, GT], F32R) for n in ("XH", "XL"))
        qkH, qkL = (sbuf(A, n, [P, 2, 4, GT], F32R) for n in ("qkH", "qkL"))
        vs = sbuf(A, "vs", [P, 2, 4, D + NE])
        Wost = vs[:, 1, 0:2, 0:D]

        def rows(w):
            return w.rearrange("(c p) n -> p c n", p=P)

        x_v = t["x"].rearrange("b s d -> (b s) d").rearrange("(g j p) d -> g p j d", p=P, j=4)
        m_x, m_norm = {}, {}

        def load_x(g):
            m_x[g] = dma("sync", f"x{g % 4}", xt[:, g % 4, :, :], x_v[g], m_norm.get(g - 4))

        load_x(0)
        dma("scalar", "c_w1", Wst[:, 0, :, :], rows(t["Wq"]))
        dma("scalar", "c_w1", Wst[:, 1, :, :], rows(t["Wk"]))
        dma("scalar", "c_w1", Wvst[:, :, 0:D], rows(t["Wv"]))
        m_w1 = dma("scalar", "c_w1", Wvst[:, :, D:D + NE], rows(t["Wg"]))
        dma("sync", "c_w", Wost, rows(t["Wo"]))
        dma("sync", "c_w", bqk[:, 0:2], t["bq"].rearrange("(m p) -> p m", p=P), slow=True)
        dma("sync", "c_w", bqk[:, 2:4], t["bk"].rearrange("(m p) -> p m", p=P), slow=True)
        m_w = dma("sync", "c_w", bvr[:, :], t["bv"].rearrange("(a n) -> a n", a=1).broadcast_to([P, D]))

        for g in range(1, 4):
            load_x(g)

        m_nhalf = pool(lambda e: e.memset(nhalf[:, :], -0.5))
        m_alibi = dma("gpsimd", "c_ali", Alid[:, :, :, :], t["c_alibi"])
        m_pad = [None] * 3

        def pad(i):
            m = ("gpsimd", pr.at["gpsimd"])
            if i == 0:
                m_pad[0] = pool(lambda e: e.memset(QO[64:96, :, :, :].bitcast(F32), 1.0), m)
            elif i == 1:
                pool(lambda e: e.memset(KO[64:96, :, :, :].bitcast(F32), 0.0), m)
            elif i == 2:
                m = pool(lambda e: e.memset(KO[96:98, :, :, :].bitcast(F32), 1.0), m)
                m_pad[1] = dma("sync", "c_one", KO[66:68, :, :, :].bitcast(F32), KO[96:98, :, :, :].bitcast(F32), m)
            elif i == 3:
                m_pad[2] = pool(lambda e: e.memset(VB[:, :], 0.0), m)
            elif i == 4:
                m_pad[2] = pool(lambda e: e.memset(
                    vb.rearrange("p b c (h d) -> p (b c) h d", d=32)[:, :, :, HD:HD + 1], 1.0), m_pad[2])

        xn_v = Xn.rearrange("(g j p) d -> g p j d", p=P, j=4)
        v_v = Vd.rearrange("(g j p) n -> g p j n", p=P, j=4)
        m_rstd, m_xnst, m_xev, m_xmm, m_qkst, m_vst, m_tr = {}, {}, {}, {}, {}, {}, {}
        free = {}
        px = [0]

        def take():
            bank = 5 + px[0] % 3
            px[0] += 1
            return bank


        m_wt = {}

        def split_weights():
            a1 = act(lambda e: e.activation(Wqk["h"][:, 0, :, :], Wst[:, 0, :, :], ACT.Copy, scale=SCALE), m_w1)
            a2 = act(lambda e: e.copy(Wqk["h"][:, 1, :, :], Wst[:, 1, :, :]))
            a3 = act(lambda e: e.copy(Wv["h"][:, :, :], Wvst[:, :, :]))
            m_wq = dve(lambda e: e.scalar_tensor_tensor(Wqk["l"][:, 0, :, :], Wst[:, 0, :, :], SCALE,
                                                        Wqk["h"][:, 0, :, :].bitcast(F32), ALU.mult, ALU.subtract), a1)
            m_wk = dve(lambda e: e.tensor_tensor(Wqk["l"][:, 1, :, :], Wst[:, 1, :, :],
                                                 Wqk["h"][:, 1, :, :].bitcast(F32), ALU.subtract), a2)
            m_wv = dve(lambda e: e.tensor_tensor(Wv["l"][:, :, :], Wvst[:, :, :], Wv["h"][:, :, :].bitcast(F32),
                                                 ALU.subtract), a3)
            m_wt.update(qk=(m_wq, m_wk), v=m_wv)

        def split_wo():
            m_bq = dve(lambda e: e.tensor_scalar(bqk[:, 0:2], bqk[:, 0:2], SCALE, None, ALU.mult), m_w)
            a4 = act(lambda e: e.copy(WoH[:, :, :], Wost), m_w)
            m_wo = dve(lambda e: e.tensor_tensor(WoL[:, :, :], Wost, WoH[:, :, :].bitcast(F32), ALU.subtract), a4)
            m_wt.update(bq=m_bq, o=m_wo)

        NPAIR = NB * NH // 2
        m_ops, m_st_last, m_a_last, m_mrow = {}, {}, {}, {}

        def load_pair(r, part=None):
            b, j = divmod(r, NH // 2)
            k = r % 3
            nm = f"op{k}"
            at = slice(b * S, (b + 1) * S)
            if part in (None, 0):
                wait("sync", m_pad[0], m_pad[1], m_alibi, m_st_last.get(r - 3), m_a_last.get(r - 3), *m_qkst[2 * b], *m_qkst[2 * b + 1])
            for i in range(4) if part is None else (part,):
                dst, o, parts, al = ((QO, 0, (QKh, QKl, QKh, QKl), 1), (KO, D, (QKh, QKh, QKl, QKl), 0))[i // 2]
                for n in (0, 1) if i % 2 == 0 else (2, 3):
                    dma("sync", nm, dst[16 * n:16 * n + 16, k, :, :].bitcast(F32),
                        parts[n][o + 32 * j:o + 32 * j + 32, at].rearrange("(h d) n -> d h n", d=HD))
                if i % 2:
                    m_ops[r] = dma("sync", nm, dst[64 + 2 * al:66 + 2 * al, k, :, :].bitcast(F32),
                                   Alid[al, 2 * j:2 * j + 2, :, :].rearrange("h r n -> r h n"))

        m_mxfree = {}

        n_unit = [0]

        def score_max(bank=None):
            r, u = divmod(n_unit[0], 32)
            if r == NPAIR:
                return
            n_unit[0] += 1
            hh, i, half = u // 16, (u // 2) % 8, u % 2
            k = r % 3
            bank = take() if bank is None else bank
            q = mm(ps[:, bank, :], QO[0:96, k, hh, i * P:(i + 1) * P], KO[0:96, k, hh, half * GT:(half + 1) * GT],
                   True, True, m_ops[r], *free.get(bank, ()), sig=True)
            d = dve(lambda e: e.reduce_max(mx[:, r % 2, hh, i, half:half + 1], ps[:, bank, :], AX.X), q)
            free[bank] = (d,)
            if u == 31:
                m_a_last[r] = q
                k2 = r % 2
                m = dve(lambda e: e.tensor_reduce(m16[:, k2, :, :], mx[:, k2, :, :, :], AX.X, ALU.max), d)
                m1 = act(lambda e: e.activation(mneg[:, k2, :, 0, :].bitcast(F32R), m16[:, k2, :, :], ACT.Copy,
                                                scale=-1.0), m, m_mxfree.get(r - 2))
                m_mrow[r] = dve(lambda e: e.scalar_tensor_tensor(mneg[:, k2, :, 1, :], m16[:, k2, :, :], -1.0,
                                                                 mneg[:, k2, :, 0, :], ALU.mult, ALU.subtract), m1)

        m_max = {}

        def max_rows(r, bank=None):
            k2 = r % 2
            bank = take() if bank is None else bank
            q = transpose(ps[0:32, bank, 0:P], mneg[:, k2, :, :, :].rearrange("p h l i -> p (h l i)"),
                          m_mrow[r], m_ident, *free[bank], sig=True)
            m_mxfree[r] = q
            d = act(lambda e: e.copy(mT[:, k2, :], ps[0:32, bank, 0:P]), q, m_max.get(r - 2))
            free[bank] = (d,)
            for hh in range(2):
                m_max[r] = dma("sync", f"mx{k2}", QO[96:98, r % 3, hh, :].bitcast(F32).rearrange("l (i n) -> l i n", n=P),
                               mT[16 * hh:16 * hh + 16, k2, :].bitcast(F32), d)

        m_v, m_vst2, m_pv_batch = {}, {}, {}
        v_rows = Vd.rearrange("(b f c p) n -> b f p c n", p=P, c=4, f=2)

        def load_v(b, f):
            i = 2 * b + f
            ld = dma("gpsimd", "vst", vst[:, :, :], v_rows[b, f], m_vst2.get(i - 1), m_vst[2 * b + f])
            m_v[b] = m_vst2[i] = pool(lambda e: e.tensor_copy(
                vb[:, b % 2, 4 * f:4 * f + 4, :].rearrange("p c (h d) -> p c h d", d=32)[:, :, :, 0:HD],
                vst[:, :, :].rearrange("p c (h d) -> p c h d", d=HD)), ld, m_pad[2], m_pv_batch.get(b - 2))

        def layer_stats(g, half):
            k = g % 2
            for j in (2 * half, 2 * half + 1):
                s = dve(lambda e, j=j: e.bn_stats(stats[:, k, j, :], xt[:, g % 4, j, :]), m_x[g])
            if half:
                wait("vector", s)
                for j in range(4):
                    s = dve(lambda e, j=j: e.bn_aggr(mv[:, k, j, :], stats[:, k, j, :]))
                s = dve(lambda e: e.tensor_scalar(veps[:, k, :], mv[:, k, :, 1], EPS, None, ALU.add), s)
                m_rstd[g] = pool(lambda e: e.tensor_tensor(rstd[:, k, :], veps[:, k, :], nhalf[:, :], ALU.pow),
                                 s, m_nhalf, ("gpsimd", pr.at["gpsimd"]))

        def normalise(g, half):
            k = g % 2
            n = g % 3
            wait("vector", m_rstd[g], m_tr.get(g - 3), m_xnst.get(g - 3))
            for j in (2 * half, 2 * half + 1):
                s = dve(lambda e, j=j: e.tensor_scalar(xn[:, n, j, :], xt[:, g % 4, j, :], mv[:, k, j, 0:1],
                                                       rstd[:, k, j:j + 1], ALU.subtract, ALU.mult))
            if half:
                m_norm[g] = s
                m_xnst[g] = dma("sync", f"xn{n}", xn_v[g], xn[:, n, :, :], s)
                if g + 4 < NG:
                    load_x(g + 4)

        def to_columns(src, banks, hi, lo, *m):
            wait("tensor", m_ident, *m, *free.get(banks[0], ()), *free.get(banks[1], ()))
            for c in range(2):
                for j in range(4):
                    tr = transpose(ps[:, banks[c], j * P:(j + 1) * P], src[:, j, c * P:(c + 1) * P],
                                   sig=c == 1 and j == 3)
            b = banks[0]
            a = act(lambda e: e.copy(hi, ps[:, b:b + 2, :]), tr)
            d = dve(lambda e: e.tensor_tensor(lo, ps[:, b:b + 2, :], hi.bitcast(F32), ALU.subtract), a)
            free[banks[0]] = free[banks[1]] = (a, d)
            return tr, (a, d)

        def columns(g):
            k = g % 2
            b = 2 * k
            wait("scalar", *m_xmm.get(g - 2, ()))
            wait("vector", *m_xmm.get(g - 2, ()))
            m_tr[g], m_xev[g] = to_columns(xn[:, g % 3, :, :], (b, b + 1), XH[:, k, :, :], XL[:, k, :, :], m_norm[g])

        ring_a = [0]

        def project(g, fills):
            k = g % 2
            wait("tensor", *m_xev[g], *m_wt["qk"], m_wt["v"])
            wait("scalar", *m_qkst.get(g - 2, ()), m_vst.get(g - 2), m_wt["bq"], m_wt["o"])
            wait("vector", *m_qkst.get(g - 2, ()), m_w)
            for o in range(4):
                bank = 4 + ring_a[0] % 3
                ring_a[0] += 1
                w, m0 = o // 2, (o % 2) * P
                q = mm3(ps[:, bank, :], [(Wqk["h"][:, w, c, m0:m0 + P], Wqk["l"][:, w, c, m0:m0 + P],
                                          XH[:, k, c, :], XL[:, k, c, :]) for c in range(2)],
                        *free.get(bank, ()), sig=True)
                a = act(lambda e, o=o, bank=bank: e.activation(qkH[:, k, o, :], ps[:, bank, :], ACT.Identity,
                                                               bias=bqk[:, o:o + 1]), q)
                d = dve(lambda e, o=o, bank=bank: e.scalar_tensor_tensor(
                    qkL[:, k, o, :], ps[:, bank, :], bqk[:, o:o + 1], qkH[:, k, o, :].bitcast(F32),
                    ALU.add, ALU.subtract), a)
                free[bank] = (a, d)
                fills[o]()
            at = slice(g * GT, (g + 1) * GT)
            s1 = dma("sync", f"qh{k}", QKh.rearrange("(o p) n -> p o n", p=P)[:, :, at], qkH[:, k, :, :].bitcast(F32), a)
            s2 = dma("sync", f"ql{k}", QKl.rearrange("(o p) n -> p o n", p=P)[:, :, at], qkL[:, k, :, :].bitcast(F32), d)
            m_qkst[g] = (s1, s2)
            for j in range(4):
                bank = 4 + ring_a[0] % 3
                ring_a[0] += 1
                q = mm3(ps[:, bank, 0:D + NE], [(XH[:, k, c, j * P:(j + 1) * P], XL[:, k, c, j * P:(j + 1) * P],
                                                 Wv["h"][:, c, :], Wv["l"][:, c, :]) for c in range(2)],
                        *free.get(bank, ()), sig=True)
                a = act(lambda e, j=j, bank=bank: e.copy(vs[:, k, j, :], ps[:, bank, 0:D + NE]), q)
                free[bank] = (a,)
                fills[4 + j]()
            m_xmm[g] = (q,)
            wait("gpsimd", ("gpsimd", pr.at["gpsimd"]))
            m = pool(lambda e: e.tensor_copy(Lg[:, 4 * g:4 * g + 4, :], vs[:, k, :, D:D + NE]), a)
            d = pool(lambda e: e.tensor_tensor(
                vs[:, k, :, 0:D], vs[:, k, :, 0:D],
                bvr[:, :].rearrange("p (u d) -> p u d", u=1).broadcast_to([P, 4, D]), ALU.add), m_w)
            m_vst[g] = dma("sync", f"vs{k}", v_v[g], vs[:, k, :, 0:D], d)
            return m

        AHEAD = 48
        FIRST = 6
        PAIR_AT = (3, 6)
        V_AT = 10
        UNITS = (0, 2, 5, 7)
        layer_stats(0, 0)
        layer_stats(0, 1)
        split_weights()
        for half in range(2):
            normalise(0, half)
        layer_stats(1, 0)
        layer_stats(1, 1)
        columns(0)
        split_wo()
        pad(0)
        layer_stats(2, 0)
        for half in range(2):
            normalise(1, half)
        layer_stats(2, 1)
        for g in range(NG):
            if g + 3 < NG:
                layer_stats(g + 3, 0)
            if g + 2 < NG:
                normalise(g + 2, 0)
            if 0 < g and g + 1 < NG:
                columns(g + 1)
            fills = [lambda: None] * 8
            if g == 0:
                fills[4] = lambda: columns(1)
            if g + 2 < NG:
                fills[1] = lambda g=g: normalise(g + 2, 1)
            if g + 3 < NG:
                fills[3] = lambda g=g: layer_stats(g + 3, 1)
            if g >= FIRST:
                for i in UNITS:
                    fills[i] = lambda f=fills[i]: (f(), score_max(7) if n_unit[0] < AHEAD else None)
            pad(g + 1)
            m_lg = project(g, fills)
            if 0 <= g - V_AT < 2:
                load_v(0, g - V_AT)
            if n_unit[0] >= 32 and 0 not in m_max:
                max_rows(0, 7)
            for r in range(2):
                if 0 <= g - PAIR_AT[r] < 2:
                    for i in range(2):
                        load_pair(r, 2 * (g - PAIR_AT[r]) + i)
        done_a = [m_lg, *m_qkst[NG - 1], *m_qkst[NG - 2], m_vst[NG - 1], m_vst[NG - 2],
                  m_xnst[NG - 1], m_xnst[NG - 2], m_xnst[NG - 3], *m_xmm[NG - 1], m_wt["o"], m_w]
        A.close()

        B = ExitStack()
        NPT = 8
        pta = sbuf(B, "pta", [P, NPT // 2, S])
        WR = [sbuf(B, f"WR{i}", [P, RAW]) for i in range(3)]
        WB0 = sbuf(B, "WB0", [P, 2 * RAW], F32R)
        ot = sbuf(B, "ot", [P, 8, D])
        ptb = sbuf(B, "ptb", [P, NPT // 2, S])
        accs = sbuf(B, "accs", [P, 2, GT])
        rc = sbuf(B, "rc", [P, 2, 4, 4])
        zero = sbuf(B, "zero", [P, D])
        R = B
        rt = {n: sbuf(R, "r_" + n, [P, NT, NE]) for n in ("eq", "o1", "o2", "t", "pa", "pb")}
        rt["rk"] = rt["eq"]
        rs = {n: sbuf(R, "r_" + n, [P, NT]) for n in ("m1", "m2", "r", "s")}
        cnt = {n: sbuf(R, "r_" + n, [P, NE]) for n in ("nb", "ia", "ib", "base")}
        cmpn = rt["t"][:, :, :].rearrange("p n e -> p (n e)")[:, 0:NE * NCMP].rearrange("p (e j) -> p e j", e=NE)
        cmpb = sbuf(R, "cmpb", [P, NBLK, NE])
        bex = sbuf(R, "bex", [P, NBLK])
        tri = sbuf(R, "tri", [P, P])
        onesm = sbuf(R, "onesm", [P, P])
        crow = sbuf(R, "crow", [P, 8 + NCMP + NBLK + 1])
        dma("gpsimd", "c_r", tri[:, :], t["c_tri"], *done_a)
        m_cr = dma("gpsimd", "c_r", crow[:, :], t["c_row"])
        m_ones = pool(lambda e: e.memset(onesm[:, :], 1.0), *done_a)
        m_zero = pool(lambda e: e.memset(zero[:, :], 0.0))
        def over_tiles(a):
            return a.rearrange("p (u e) -> p u e", u=1).broadcast_to([P, NT, NE])

        def over_experts(a):
            return a.rearrange("p (n u) -> p n u", u=1).broadcast_to([P, NT, NE])

        rev = over_tiles(crow[:, 0:8])

        def tt(o, a, b, op, *m):
            return dve(lambda e: e.tensor_tensor(o, a, b, op), *m)

        def red(o, a, op, *m):
            return dve(lambda e: e.tensor_reduce(o, a, AX.X, op), *m)

        def first_of(best, one_hot, logits, m):
            m = red(best, logits, ALU.max, m)
            yield
            m = tt(rt["eq"][:, :, :], logits, over_experts(best), ALU.is_equal, m)
            yield
            m = tt(rt["t"][:, :, :], rt["eq"][:, :, :], rev, ALU.mult, m)
            yield
            m = red(rs["r"][:, :], rt["t"][:, :, :], ALU.max, m)
            yield
            return tt(one_hot, rt["t"][:, :, :], over_experts(rs["r"][:, :]), ALU.is_equal, m)

        routed = {}

        def route():
            wait("vector", *done_a, m_cr)
            m = yield from first_of(rs["m1"][:, :], rt["o1"][:, :, :], Lg[:, :, :], None)
            yield
            m = dve(lambda e: e.scalar_tensor_tensor(rt["pa"][:, :, :], rt["o1"][:, :, :], -3.0e38, Lg[:, :, :],
                                                     ALU.mult, ALU.add), m)
            yield
            m = yield from first_of(rs["m2"][:, :], rt["o2"][:, :, :], rt["pa"][:, :, :], m)
            yield
            m_d = tt(rs["s"][:, :], rs["m2"][:, :], rs["m1"][:, :], ALU.subtract, m)
            yield
            m_e = act(lambda e: e.activation(rs["s"][:, :], rs["s"][:, :], ACT.Exp), m_d)
            yield
            m_m = tt(rt["eq"][:, :, :], rt["o1"][:, :, :], rt["o2"][:, :, :], ALU.add, m)
            yield
            m = dve(lambda e: e.tensor_scalar(rs["r"][:, :], rs["s"][:, :], 1.0, None, ALU.add), m_e, m_m)
            yield
            m = dve(lambda e: e.reciprocal(prob[:, 0, :], rs["r"][:, :]), m)
            yield
            routed["prob"] = tt(prob[:, 1, :], rs["s"][:, :], prob[:, 0, :], ALU.mult, m)
            flat = rt["eq"][:, :, :].rearrange("p n e -> p (n e)")
            bk0, bk1 = take(), take()
            mm(ps[:, bk0, :], tri[:, :], flat, True, True, m_m, m_cr, m_ones, *free[bk0])
            mr = mm(ps[:, bk1, :], onesm[:, :], flat, True, True, *free[bk1], sig=True)
            b0 = ps[:, bk0, :].rearrange("p (n e) -> p n e", e=NE)
            b1 = ps[:, bk1, :].rearrange("p (n e) -> p n e", e=NE)
            m = dve(lambda e: e.tensor_copy(rt["rk"][:, :, :], b0), mr)
            free[bk0] = (m,)
            dve(lambda e: e.tensor_copy(rt["pa"][:, :, :], b1))
            m = tt(rt["rk"][:, :, :], rt["rk"][:, :, :], b1, ALU.subtract, m)
            free[bk1] = (m,)
            a, b = rt["pa"], rt["pb"]
            sh = 1
            while sh < NT:
                m = dve(lambda e, a=a, b=b, sh=sh: e.tensor_copy(b[:, 0:sh, :], a[:, 0:sh, :]), m)
                yield
                m = tt(b[:, sh:NT, :], a[:, sh:NT, :], a[:, 0:NT - sh, :], ALU.add, m)
                yield
                a, b = b, a
                sh *= 2
            total = a[:, NT - 1, :]
            m2 = tt(cmpn[:, :, :], total.rearrange("p (e u) -> p e u", u=1).broadcast_to([P, NE, NCMP]),
                    crow[:, 8:8 + NCMP].rearrange("p (u j) -> p u j", u=1).broadcast_to([P, NE, NCMP]), ALU.is_gt, m)
            yield
            m2 = red(cnt["nb"][:, :], cmpn[:, :, :], ALU.add, m2)
            yield
            ia, ib = cnt["ia"], cnt["ib"]
            m2 = dve(lambda e: e.tensor_copy(cnt["ia"][:, :], cnt["nb"][:, :]), m2)
            yield
            sh = 1
            while sh < NE:
                m2 = dve(lambda e, ia=ia, ib=ib, sh=sh: e.tensor_copy(ib[:, 0:sh], ia[:, 0:sh]), m2)
                yield
                m2 = tt(ib[:, sh:NE], ia[:, sh:NE], ia[:, 0:NE - sh], ALU.add, m2)
                yield
                ia, ib = ib, ia
                sh *= 2
            m3 = tt(cnt["base"][:, :], ia[:, :], cnt["nb"][:, :], ALU.subtract, m2)
            yield
            m4 = tt(cmpb[:, :, :], crow[:, 8 + NCMP:8 + NCMP + NBLK].rearrange("p (b u) -> p b u", u=1).broadcast_to([P, NBLK, NE]),
                    ia[:, :].rearrange("p (u e) -> p u e", u=1).broadcast_to([P, NBLK, NE]), ALU.is_ge, m3)
            yield
            m4 = red(bex[:, :], cmpb[:, :, :], ALU.add, m4)
            yield
            m4 = dve(lambda e: e.tensor_scalar(bex[:, :], bex[:, :], float(NE - 1), float(P), ALU.min, ALU.mult), m4)
            yield
            routed["widx"] = dve(lambda e: e.tensor_scalar(widx[:, :], bex[:, :], crow[:, 8 + NCMP + NBLK:9 + NCMP + NBLK], None, ALU.add), m4)
            m = tt(b[:, :, :], a[:, :, :], rt["rk"][:, :, :], ALU.add, m4)
            yield
            m = dve(lambda e, b=b: e.scalar_tensor_tensor(b[:, :, :], over_tiles(cnt["base"][:, :]), float(BT), b[:, :, :],
                                                          ALU.mult, ALU.add), m)
            yield
            m = tt(rt["t"][:, :, :], b[:, :, :], rt["o1"][:, :, :], ALU.mult, m)
            yield
            m = red(rs["m1"][:, :], rt["t"][:, :, :], ALU.add, m)
            yield
            m = dve(lambda e: e.tensor_copy(slot[:, 0, :], rs["m1"][:, :]), m)
            yield
            m = tt(rt["t"][:, :, :], b[:, :, :], rt["o2"][:, :, :], ALU.mult, m)
            yield
            m = red(rs["m2"][:, :], rt["t"][:, :, :], ALU.add, m)
            yield
            routed["slot"] = dve(lambda e: e.tensor_copy(slot[:, 1, :], rs["m2"][:, :]), m)

        def scatter_group(g, last=[None, None]):
            k = g % 2
            ld = dma("gpsimd", f"xg{k}", xr[:, k, :, :], xn_v[g], last[k], *done_a)
            wait("gpsimd", ld, routed["slot"], m_zs[0])
            nm = f"sc{k}"
            s = pr.sem(nm)
            for i in range(4):
                for c in range(2):
                    pr.at[nm] += 16
                    pr.queues["gpsimd"].append(lambda e, i=i, c=c: e.indirect_dma_start(
                        Xs[:, :], bass.IndirectOffsetOnAxis(ap=slot[:, c, 4 * g + i:4 * g + i + 1], axis=0),
                        xr[:, k, i, :], None).then_inc(s, 16))
            last[k] = (nm, pr.at[nm])
            m_scat[k] = last[k]

        m_scat, m_zs = [None, None], [None]

        def clear_slots(b):
            m_zs[0] = dma("gpsimd", "zero", Xs[b * BT:(b + 1) * BT, :].rearrange("(p j) d -> p j d", p=P),
                          zero[:, :].rearrange("p (u d) -> p u d", u=1).broadcast_to([P, 2, D]), m_zero)

        def wsource(e):
            if e < NE:
                return t["W1"][e], t["W2"][e], t["W3"][e]
            a = (e - NE) * HE
            return t["Ws1"][:, a:a + HE], t["Ws2"][:, a:a + HE], t["Ws3"][a:a + HE, :]

        m_wd = {}

        def pack_expert(e):
            w1, w2, w3 = wsource(e)
            d = Wd[e * P:(e + 1) * P, :]
            dma("gpsimd", "wd", d[:, 0:W2_AT].rearrange("p (c n) -> p c n", c=2), rows(w1))
            dma("gpsimd", "wd", d[:, W2_AT:W3_AT].rearrange("p (c n) -> p c n", c=2), rows(w2))
            dma("gpsimd", "wd", d[:, W3_AT:W3_AT + 2 * D].rearrange("p (c n) -> p c n", c=2), rows(w3[0:2 * P, :]))
            dma("gpsimd", "wd", d[0:96, W3_AT + 2 * D:RAW], w3[2 * P:HE, :])
            m_wd[e] = dma("gpsimd", "wd", d[96:P, W3_AT + 2 * D:RAW], zero[0:32, :], m_zero)

        def pt(s):
            return pta[:, s, :] if s < NPT // 2 else ptb[:, s - NPT // 2, :]

        m_exp, m_pv, m_pfree, m_acc = {}, {}, {}, {}
        n_exp = [0]
        p_of = {}

        def scores(r, kc, hh, half):
            k = r % 3
            n = n_exp[0]
            b0_ = 2 * (n % 2)
            q = mm(ps[:, b0_ + half, :], KO[0:98, k, hh, kc * P:(kc + 1) * P], QO[0:98, k, hh, half * GT:(half + 1) * GT],
                   True, True, m_ops[r], m_max[r], *free[b0_ + half], sig=half == 1)
            if half == 0:
                return
            n_exp[0] += 1
            if kc == 7 and hh == 1:
                m_st_last[r] = q
            s = n % NPT
            p_of[r, kc, hh] = s
            a = act(lambda e: e.activation(pt(s), ps[:, b0_:b0_ + 2, :], ACT.Exp), q, m_pfree.get(s),
                    *(done_a if s >= NPT // 2 else ()))
            free[b0_] = free[b0_ + 1] = (a,)
            m_exp[r, kc, hh] = a

        def values(r, kc):
            b, j = divmod(r, NH // 2)
            wait("tensor", m_exp[r, kc, 0], m_exp[r, kc, 1], m_v[b], *(free[4] if kc == 0 else ()))
            for hh in range(2):
                for half in range(2):
                    g4 = 2 * hh + half
                    q = mm(ps[32 * g4:32 * g4 + 32, 4, :], vb[:, b % 2, kc, 32 * (2 * j + hh):32 * (2 * j + hh) + 32],
                           pt(p_of[r, kc, hh])[:, half * GT:(half + 1) * GT], kc == 0, kc == 7, sig=g4 == 3)
            for hh in range(2):
                m_pfree[p_of[r, kc, hh]] = q
            if kc == 7:
                m_pv_batch[b] = q
                k2 = r % 2
                a = act(lambda e: e.copy(accs[:, k2, :], ps[:, 4, :]), q, m_acc.get(r - 2), *done_a)
                free[4] = (a,)
                m_pv[r] = a

        m_ot, m_od = {}, {}

        def normalise_heads(r):
            b, j = divmod(r, NH // 2)
            k2 = r % 2
            bank = take()
            wait("tensor", m_pv[r], *free[bank])
            for c in range(4):
                q = transpose(ps[:, bank, c * P:(c + 1) * P], accs[:, k2, c * P:(c + 1) * P], sig=c == 3)
            a = act(lambda e: e.copy(accs[:, k2, :], ps[:, bank, :]), q)
            free[bank] = (a,)
            v = accs[:, k2, :].rearrange("p (c g d) -> p c g d", c=4, g=4)
            m = dve(lambda e: e.reciprocal(rc[:, k2, :, :], v[:, :, :, HD]), a)
            wait("gpsimd", m, m_od.get(b - 1))
            for hh in range(2):
                h = 2 * j + hh
                o = ot[:, :, HD * h:HD * h + HD].rearrange("p (f c) d -> p c f d", f=2)
                m = pool(lambda e, hh=hh, o=o: e.tensor_tensor(
                    o, v[:, :, 2 * hh:2 * hh + 2, 0:HD],
                    rc[:, k2, :, 2 * hh:2 * hh + 2].rearrange("p c (g u) -> p c g u", u=1).broadcast_to([P, 4, 2, HD]),
                    ALU.mult))
            m_acc[r] = m
            if j == NH // 2 - 1:
                m_od[b] = dma("sync", "od", Od.rearrange("(b c p) d -> b p c d", p=P, c=8)[b],
                              ot[:, :, :], m)

        while n_unit[0] < AHEAD:
            score_max()
        load_pair(2)
        routing = route()

        ORDER = "SSuSSuuPuSSuSSuuPu"
        MAXU, NU = 7, 4

        def b_step(s):
            r, kc = divmod(s, 8)
            if s % 2 == 0:
                n = u = v = 0
                for c in ORDER:
                    if c == "S":
                        if r < NPAIR:
                            scores(r, kc + n // 4, n // 2 % 2, n % 2)
                        n += 1
                    elif c == "u":
                        score_max()
                        u += 1
                        if u == MAXU and kc == 4 and r + 1 < NPAIR:
                            max_rows(r + 1)
                        if u == NU and kc == 2 and r >= 1:
                            normalise_heads(r - 1)
                    else:
                        if s >= 2:
                            values(*divmod(s - 2 + v, 8))
                        v += 1
            if kc == 0 and r >= 1 and r + 2 < NPAIR:
                load_pair(r + 2)
            if r < NE + 2 and kc == 1:
                pack_expert(r)
            if s < NBLK:
                clear_slots(s)
            if kc == 3 and 34 <= r < 34 + NG:
                scatter_group(r - 34)
            if kc == 5 and r % 8 in (2, 3) and r < NPAIR - 8:
                load_v(r // 8 + 1, r % 8 - 2)
            if s % 4 == 3:
                next(routing, None)

        for s in range(8 * NPAIR - 8):
            b_step(s)
        for _ in routing:
            pass
        m_slot, m_widx, m_prob = routed["slot"], routed["widx"], routed["prob"]
        B.close()

        C = ExitStack()
        OH, OL = (sbuf(C, n, [P, 2, GT], F32R) for n in ("OH", "OL"))
        sbuf(C, "spare", [P, 2048])
        WR = [sbuf(C, f"WR{i}c", [P, RAW]) for i in range(3)]
        WB = [sbuf(C, "WB0c", [P, 2 * RAW], F32R)]
        gath = sbuf(C, "gath", [P, 4, 2, D])
        WB += [sbuf(C, f"WB{i}", [P, 2 * RAW], F32R) for i in (1, 2)]
        CH = OPS[:, 8192:10240].rearrange("p (b c n) -> p b c n", b=2, c=2)
        CL = OPS[:, 10240:12288].rearrange("p (b c n) -> p b c n", b=2, c=2)
        HH = OPS[:, 0:4096].rearrange("p (s n) -> p s n", s=8)
        HL = OPS[:, 4096:8192].rearrange("p (s n) -> p s n", s=8)
        orow = VB[:, 0:1024].rearrange("p (j d) -> p j d", j=4)
        sg = VB[:, 1024:2048].rearrange("p (b n) -> p b n", b=2)
        hf = VB[:, 2048:3072].rearrange("p (b n) -> p b n", b=2)
        yr = VB[:, 3072:5120].rearrange("p (b j d) -> p b j d", b=2, j=4)
        xres = VB[:, 5120:6144].rearrange("p (j d) -> p j d", j=4)
        gu = [0]
        nh = [0]
        m_wb, m_wbfree, m_xr, m_xcol, m_xused, m_xrfree = {}, {}, {}, {}, {}, {}
        m_h, m_hfree, m_sg, m_hf = {}, {}, {}, {}

        sgq = VB[:, 1024:2048].rearrange("p (b n) -> p b n", b=4)
        hfq = VB[:, 2048:3072].rearrange("p (b n) -> p b n", b=4)

        def operands(xh, xl, w, at, hn):
            return [(w[:, at + c * HE:at + c * HE + hn], w[:, RAW + at + c * HE:RAW + at + c * HE + hn],
                     xh[:, c, :], xl[:, c, :]) for c in range(2)]

        def gate_up_block(xh, xl, w, hc, between, *m):
            h0, hn = HC[hc]
            n = nh[0]
            nh[0] += 1
            s, k, bank = n % 8, n % 4, 2 + n % 4
            wait("tensor", *m)
            mm3(ps[0:hn, bank, 0:BT], operands(xh, xl, w, h0, hn), *free[bank])
            q = mm3(ps[0:hn, bank, BT:2 * BT], operands(xh, xl, w, W2_AT + h0, hn), sig=True)
            a_ = act(lambda e: e.activation(sgq[0:hn, k, :], ps[0:hn, bank, 0:BT], ACT.Silu), q, m_hf.get(n - 4))
            d = dve(lambda e: e.tensor_tensor(hfq[0:hn, k, :], ps[0:hn, bank, BT:2 * BT], sgq[0:hn, k, :], ALU.mult),
                    a_, *m_h.get(n - 4, ()))
            free[bank] = (d,)
            m_hf[n] = d
            between()
            a2 = act(lambda e: e.copy(HH[0:hn, s, 0:BT], hfq[0:hn, k, :]), d, m_hfree.get(s))
            d2 = dve(lambda e: e.tensor_tensor(HL[0:hn, s, 0:BT], hfq[0:hn, k, :], HH[0:hn, s, 0:BT].bitcast(F32),
                                               ALU.subtract), a2)
            m_h[n] = (a2, d2)
            return n

        def gate_up(xh, xl, w, hc, *m):
            h0, hn = HC[hc]
            n = nh[0]
            nh[0] += 1
            s, k = n % 8, n % 2
            last = n - 2 if n >= 3 * NBLK + 2 else 3 * NBLK - 1
            banks = (2 + 2 * (n % 2), 3 + 2 * (n % 2))
            wait("tensor", *m)
            for which, bank in zip((0, W2_AT), banks):
                q = mm3(ps[0:hn, bank, :], operands(xh, xl, w, which + h0, hn), *free[bank], sig=True)
                if which == 0:
                    a_ = act(lambda e: e.activation(sg[0:hn, k, :], ps[0:hn, banks[0], :], ACT.Silu), q, m_hf[last])
                    free[banks[0]] = (a_,)
            d = dve(lambda e: e.tensor_tensor(hf[0:hn, k, :], ps[0:hn, banks[1], :], sg[0:hn, k, :], ALU.mult),
                    q, a_, *m_h[last])
            free[banks[1]] = (d,)
            m_hf[n] = d
            a2 = act(lambda e: e.copy(HH[0:hn, s, :], hf[0:hn, k, :]), d, m_hfree.get(s))
            d2 = dve(lambda e: e.tensor_tensor(HL[0:hn, s, :], hf[0:hn, k, :], HH[0:hn, s, :].bitcast(F32),
                                               ALU.subtract), a2)
            m_h[n] = (a2, d2)
            return n

        def down(chunks, extra=()):
            for j in range(4):
                col = slice(j * P, (j + 1) * P)
                ks = []
                for w, hc, n in chunks:
                    hn = HC[hc][1]
                    a = W3_AT + hc * D
                    wait("tensor", *m_h[n])
                    ks.append((HH[0:hn, n % 8, col], HL[0:hn, n % 8, col], w[0:hn, a:a + D], w[0:hn, RAW + a:RAW + a + D]))
                for xh, xl, wh, wl in extra:
                    ks.append((xh[:, col], xl[:, col], wh, wl))
                q = mm3(ps[:, 6 + j // 2, (j % 2) * D:(j % 2) * D + D], ks, *free[6 + j // 2], sig=j == 3)
            for _, _, n in chunks:
                m_hfree[n % 8] = q
            return q

        m_yr = {}
        xs_v = Xs.rearrange("(b j p) d -> b p j d", p=P, j=2)
        ys_v = Ys.rearrange("(b j p) d -> b p j d", p=P, j=2)

        m_ws, m_wpiece = {}, {}
        PIECES = ((0, W2_AT), (W2_AT, W3_AT), (W3_AT, RAW))

        def gather_weights(b):
            k = b % 3
            nm = f"wb{k}"
            if b >= NBLK:
                e0 = (NE + b - NBLK) * P
                m_wb[b] = dma("gpsimd", nm, WR[k][:, :], Wd[e0:e0 + P, :], *m_ws[b - 3])
                return
            wait("gpsimd", m_widx, *m_ws.get(b - 3, ()), m_wd[NE + 1])
            s = pr.sem(nm)
            pr.at[nm] += 16
            pr.queues["gpsimd"].append(lambda e: e.indirect_dma_start(
                WR[k][:, :], None, Wd[:, :],
                bass.IndirectOffsetOnAxis(ap=widx[:, b:b + 1], axis=0)).then_inc(s, 16))
            m_wb[b] = (nm, pr.at[nm])

        def split_weights_of(b, i):
            if b > NBLK + 1:
                return
            r, w = WR[b % 3], WB[b % 3]
            lo, hi = PIECES[i]
            a = act(lambda e: e.copy(w[:, lo:hi], r[:, lo:hi]), m_wb[b], m_wbfree.get(b - 3),
                    *((m_pv[NPAIR - 1], m_acc[NPAIR - 1], m_zs[0], m_wd[NE + 1]) if b in (1, 2) else ()))
            eng = "gpsimd" if i == 0 else "vector"
            d = put(eng, lambda e: e.tensor_tensor(w[:, RAW + lo:RAW + hi], r[:, lo:hi], w[:, lo:hi].bitcast(F32),
                                                   ALU.subtract), a)
            m_wpiece[b, i] = (a, d)
            if i == 2:
                m_ws[b] = (*m_wpiece[b, 0], a, d)

        def xslot(b):
            return xr[:, b // 2 % 2, 2 * (b % 2):2 * (b % 2) + 2, :]

        def load_slots(b):
            m_xr[b] = dma("sync", f"xs{b % 4}", xslot(b), xs_v[b], m_xrfree.get(b - 4), *m_scat, m_zs[0])

        def slot_columns(b):
            k = b % 2
            wait("scalar", m_xused.get(b - 2))
            wait("vector", m_xused.get(b - 2))
            if b >= NBLK:
                m_xrfree[b], m_xcol[b] = to_columns(xr[:, k, :, :], (0, 1), CH[:, k, :, :], CL[:, k, :, :], m_xr[b])
                return
            wait("tensor", m_xr[b], *free[k])
            for c in range(2):
                for j in range(2):
                    tr = transpose(ps[:, k, (2 * c + j) * P:(2 * c + j + 1) * P], xslot(b)[:, j, c * P:(c + 1) * P],
                                   sig=c == 1 and j == 1)
            v = ps[:, k, :].rearrange("p (c n) -> p c n", c=2)
            a = act(lambda e: e.copy(CH[:, k, :, 0:BT], v), tr)
            d = dve(lambda e: e.tensor_tensor(CL[:, k, :, 0:BT], v, CH[:, k, :, 0:BT].bitcast(F32), ALU.subtract), a)
            free[k] = (a, d)
            m_xrfree[b], m_xcol[b] = tr, (a, d)

        h_of = {}

        def block_up(b, hc):
            k = b % 2
            h_of[b, hc] = gate_up_block(CH[:, k, :, 0:BT], CL[:, k, :, 0:BT], WB[b % 3], hc,
                                        lambda: split_weights_of(b + 1, hc) if b or hc else None, *m_xcol[b],
                                        *m_wpiece[b, 0], *m_wpiece[b, 1])
            m_xused[b] = ("tensor", pr.at["tensor"])

        def block_down(b):
            bank = 6 + b % 2
            k = b % 2
            w = WB[b % 3]
            wait("tensor", *m_wpiece[b, 2], *free[bank])
            for j in range(2):
                ks = []
                for hc in range(3):
                    n, hn, a = h_of[b, hc], HC[hc][1], W3_AT + hc * D
                    wait("tensor", *m_h[n])
                    ks.append((HH[0:hn, n % 8, j * P:(j + 1) * P], HL[0:hn, n % 8, j * P:(j + 1) * P],
                               w[0:hn, a:a + D], w[0:hn, RAW + a:RAW + a + D]))
                q = mm3(ps[:, bank, j * D:(j + 1) * D], ks, sig=j == 1)
            for hc in range(3):
                m_hfree[h_of[b, hc] % 8] = q
            m_wbfree[b] = q
            a = act(lambda e: e.copy(yr[:, k, 0:2, :].rearrange("p j d -> p (j d)"), ps[:, bank, :]), q, m_yr.get(b - 2))
            free[bank] = (a,)
            m_yr[b] = dma("sync", f"yr{k}", ys_v[b], yr[:, k, 0:2, :], a)

        od_v = Od.rearrange("(g j p) d -> g p j d", p=P, j=4)
        out_v = out.rearrange("b s d -> (b s) d").rearrange("(g j p) d -> g p j d", p=P, j=4)
        m_xr2, m_or, m_orfree, m_oc, m_gf, m_g, m_res, m_resf = {}, {}, {}, {}, {}, {}, {}, {}
        base = NBLK

        def load_rows(g):
            k = (base + g) % 2
            m_xr[base + g] = dma("sync", f"xr{k}", xr[:, k, :, :], xn_v[g],
                                 m_xrfree[base + g - 2 if g >= 2 else base - 1])

        def load_o(g):
            m_or[g] = dma("sync", "or", orow, od_v[g], m_orfree.get(g - 1) if g else m_pv[NPAIR - 1], m_od[NB - 1])

        def o_columns(g):
            wait("scalar", m_xused.get(base + g - 1))
            wait("vector", m_xused.get(base + g - 1), )
            if g == 0:
                wait("scalar", *done_b)
                wait("vector", *done_b)
            wait("scalar", m_ydone.get(g - 1))
            wait("vector", m_ydone.get(g - 1))
            m_orfree[g], m_oc[g] = to_columns(orow, (0, 1), OH[:, :, :], OL[:, :, :], m_or[g])

        m_ydone = {}
        m_out = {}

        def gather_rows(g, j):
            i = 4 * g + j
            wait("gpsimd", m_yr[NBLK - 1], m_yr[NBLK - 2], m_gf.get(i - 4), m_prob)
            nm = f"ga{j}"
            for c in range(2):
                s = pr.sem(nm)
                pr.at[nm] += 16
                pr.queues["gpsimd"].append(lambda e, c=c, s=s: e.indirect_dma_start(
                    gath[:, j, c, :], None, Ys[:, :],
                    bass.IndirectOffsetOnAxis(ap=slot[:, c, i:i + 1], axis=0)).then_inc(s, 16))
            m_g[i] = (nm, pr.at[nm])

        def load_res(g):
            m_res[g] = dma("sync", "res", xres, x_v[g], m_resf.get(g - 1) if g else m_pv[NPAIR - 1])

        def shared_up(g, e, hc):
            k = (base + g) % 2
            h_of[base + g, e, hc] = gate_up(CH[:, k, :, :], CL[:, k, :, :], WB[(NBLK + e) % 3], hc, *m_xcol[base + g],
                                                *m_wpiece[NBLK + e, 0], *m_wpiece[NBLK + e, 1])
            m_xused[base + g] = ("tensor", pr.at["tensor"])

        def shared_down(g):
            wait("tensor", *m_wpiece[NBLK, 2], *m_wpiece[NBLK + 1, 2])
            q = down([(WB[(NBLK + e) % 3], hc, h_of[base + g, e, hc]) for e in range(2) for hc in range(3)],
                     [(OH[:, c, :], OL[:, c, :], WoH[:, c, :], WoL[:, c, :]) for c in range(2)])
            m_ydone[g] = q
            k = g % 2
            wait("vector", q, m_yr.get(base + g - 2), m_prob)
            for j in range(4):
                i = 4 * g + j
                s1 = dve(lambda e, j=j, i=i: e.scalar_tensor_tensor(
                    yr[:, k, j, :], gath[:, j, 0, :], prob[:, 0, i:i + 1], ps[:, 6 + j // 2, (j % 2) * D:(j % 2) * D + D],
                    ALU.mult, ALU.add), m_g[i])
            free[6] = free[7] = (s1,)
            wait("vector", s1)
            for j in range(4):
                i = 4 * g + j
                m_gf[i] = dve(lambda e, j=j, i=i: e.scalar_tensor_tensor(
                    yr[:, k, j, :], gath[:, j, 1, :], prob[:, 1, i:i + 1], yr[:, k, j, :], ALU.mult, ALU.add))
            b = pool(lambda e: e.tensor_tensor(xres, xres, bor[:, :].rearrange("p (u d) -> p u d", u=1).broadcast_to(
                [P, 4, D]), ALU.add), m_res[g], m_bor)
            a = put("vector" if g == NG - 1 else "gpsimd",
                    lambda e: e.tensor_tensor(yr[:, k, :, :], yr[:, k, :, :], xres, ALU.add), m_gf[4 * g + 3], b)
            m_resf[g] = a
            m_yr[base + g] = m_out[g] = dma("sync", f"yr{k}", out_v[g], yr[:, k, :, :], a)

        for b in range(3):
            gather_weights(b)
            load_slots(b)
        for s in range(8 * NPAIR - 8, 8 * NPAIR):
            b_step(s)
            if s % 8 in (2, 4, 6):
                split_weights_of(0, s % 8 // 2 - 1)
        slot_columns(0)
        for s in range(8 * NPAIR, 8 * NPAIR + 2):
            b_step(s)
        block_up(0, 0)
        normalise_heads(NPAIR - 1)
        done_b = [m_od[NB - 1], m_pv[NPAIR - 1], m_acc[NPAIR - 1], m_v[NB - 1]]
        split_weights_of(1, 0)
        for b in range(NBLK):
            if b:
                block_up(b, 0)
            if b < NBLK - 1:
                slot_columns(b + 1)
            block_up(b, 1)
            if b:
                block_down(b - 1)
            if b == NBLK - 1:
                slot_columns(b + 1)
            block_up(b, 2)
            if b + 3 <= NBLK + 1:
                gather_weights(b + 3)
            if b + 3 < NBLK:
                load_slots(b + 3)
            if b == NBLK - 2:
                load_rows(0)
                load_rows(1)
                load_o(0)
                load_res(0)
        shared_up(0, 0, 0)
        block_down(NBLK - 1)
        for i in range(3):
            split_weights_of(NBLK + 1, i)
        for j in range(4):
            gather_rows(0, j)
        for g in range(NG + 1):
            if 0 < g < NG:
                shared_up(g, 0, 0)
            if g >= 1:
                shared_down(g - 1)
            if g < NG:
                shared_up(g, 0, 1)
                o_columns(g)
                shared_up(g, 0, 2)
            if 1 <= g < NG:
                load_res(g)
                for j in range(4):
                    gather_rows(g, j)
            if g < NG:
                if g + 1 < NG:
                    load_o(g + 1)
                shared_up(g, 1, 0)
                if g + 1 < NG:
                    slot_columns(base + g + 1)
                shared_up(g, 1, 1)
                shared_up(g, 1, 2)
                if g + 2 < NG:
                    load_rows(g + 2)
        wait("sync", m_out[NG - 1], m_out[NG - 2])
        C.close()
        block = ctx.enter_context(nc.Block())
        pr.emit(block)


def constants():
    slopes = (1.0 / 2.0 ** (np.arange(NH, dtype=np.float32) / NH)).astype(np.float32)
    k = np.arange(S, dtype=np.float32) - (S - 1)
    alibi = np.stack([slopes[:, None] * k[None, :], slopes[:, None] * -k[None, :]]).astype(np.float32)
    first = (alibi.view(np.uint32) & np.uint32(0xFFFFF000)).view(np.float32)
    alibi = np.stack([first, alibi - first], axis=2)
    tri = np.triu(np.ones((P, P), np.float32), 1)
    row = np.concatenate([8.0 - np.arange(8), float(BT) * np.arange(NCMP), np.arange(NBLK), [0.0]]).astype(np.float32)
    row = np.tile(row[None, :], (P, 1))
    row[:, -1] = np.arange(P)
    return {"c_ident": np.eye(P, dtype=np.float32), "c_alibi": alibi, "c_tri": tri, "c_row": row}


_NAMES = {"L0_attn_x": "x", "L0_attn_Wq": "Wq", "L0_attn_bq": "bq", "L0_attn_Wk": "Wk", "L0_attn_bk": "bk",
          "L0_attn_Wv": "Wv", "L0_attn_bv": "bv", "L0_attn_Wo": "Wo", "L0_attn_bo": "bo", "L0_ffn_Wg": "Wg",
          "L0_ffn_W1": "W1", "L0_ffn_W2": "W2", "L0_ffn_W3": "W3", "L0_ffn_Ws1": "Ws1", "L0_ffn_Ws2": "Ws2",
          "L0_ffn_Ws3": "Ws3"}


def kernel(**inputs):
    import concourse.bacc as _bacc
    from concourse.bass_utils import run_bass_kernel_spmd as _run

    nc = _bacc.Bacc("TRN2", target_bir_lowering=False, num_devices=1)
    arrays, t = {}, {}
    named = {short: np.ascontiguousarray(inputs[name]) for name, short in _NAMES.items()}
    named.update(constants())
    for short, a in named.items():
        arrays[f"in_{short}"] = a
        t[short] = nc.dram_tensor(f"in_{short}", a.shape, mybir.dt.from_np(a.dtype), kind="ExternalInput").ap()
    out = nc.dram_tensor("out_0", (NB, S, D), F32, kind="ExternalOutput").ap()
    build(nc, t, out)
    r = _run(nc, [arrays], core_ids=[0])
    return r.results[0]["out_0"]
```
